# Optimizing a Trainium2 kernel written in Bass

```python
import numpy as np
import jax
import jax.numpy as jnp

def _softmax(x, axis=-1):
    return jax.nn.softmax(x, axis=axis)

def _gelu(x):
    return jax.nn.gelu(x, approximate=True)

def _silu(x):
    return jax.nn.silu(x)

def _sigmoid(x):
    return jax.nn.sigmoid(x)

def _layernorm(x, axis=-1, eps=1e-05):
    m = jnp.mean(x, axis=axis, keepdims=True)
    v = jnp.var(x, axis=axis, keepdims=True)
    return (x - m) / jnp.sqrt(v + eps)

def _scatter_add(tgt, idx, src, axis=0):
    return tgt.at[idx].add(src)

def _segment_sum(src, seg, n):
    return jax.ops.segment_sum(src, seg, n)
kernel_name = 'mk_seq_preln_d1_jaxref_r8_6f34af'

def setup_inputs(seed: int=0):
    np.random.seed(seed)
    _w = jnp.asarray

    def _L0_attn_setup():
        import jax, jax.numpy as jnp
        import numpy as np
        B, T, D_IN = (8, 512, 256)
        D_HIDDEN = 256
        D_OUT = 256
        N_BLOCKS = 8
        R_MIN, R_MAX = (0.9, 0.999)
        INIT_IMAG = 0.1

        def _lecun(key, shape, fan_in):
            return (jax.random.normal(key, shape, dtype=jnp.float32) * np.sqrt(1.0 / fan_in)).astype(jnp.float32)

        def _block_diag_linear(x, W, b):
            h, i, j = W.shape
            xb = x.reshape(x.shape[0], x.shape[1], h, i)
            y = jnp.einsum('bthi,hij->bthj', xb, W) + b
            return y.reshape(y.shape[0], y.shape[1], h * j)

        def _linear_scan(a, x):

            def combine(l, r):
                al, bl = l
                ar, br = r
                return (al * ar, ar * bl + br)
            _, h = jax.lax.associative_scan(combine, (a, x), axis=1)
            return h

        def _reference_tuple_inner(x, W_in, b_in, W_gx, b_gx, W_ga, b_ga, a_real, a_imag, W_out, b_out):
            xh = x @ W_in + b_in
            gate_x = jax.nn.sigmoid(_block_diag_linear(xh, W_gx, b_gx))
            gate_a = jax.nn.sigmoid(_block_diag_linear(xh, W_ga, b_ga))
            log_a_re = -8.0 * gate_a * jax.nn.softplus(a_real)
            log_a_im = a_imag * gate_a
            a = jnp.exp(jax.lax.complex(log_a_re, log_a_im))
            a_sq = jnp.exp(jax.lax.complex(2.0 * log_a_re, 2.0 * log_a_im))
            xr, xi = jnp.split(xh, 2, axis=-1)
            xc = jax.lax.complex(xr, xi) * gate_x
            xc = jnp.sqrt(1.0 - a_sq) * xc
            h = _linear_scan(a, xc)
            h_m = jnp.concatenate([h.real, h.imag], axis=-1)
            out = h_m @ W_out + b_out
            h_last = h_m[:, -1]
            return (out, h_last)
        key = jax.random.key(seed)
        ks = jax.random.split(key, 12)
        dh2 = D_HIDDEN // 2
        bin_, bout = (dh2 // N_BLOCKS, None)
        blk_in = D_HIDDEN // N_BLOCKS
        blk_out = dh2 // N_BLOCKS
        u1 = jax.random.uniform(ks[8], (dh2,))
        a_r = 0.5 * jnp.log(u1 * (R_MAX ** 2 - R_MIN ** 2) + R_MIN ** 2 + 1e-08)
        a_real = jnp.log(jnp.exp(-a_r) - 1.0)
        u2 = jax.random.uniform(ks[9], (dh2,))
        a_imag = jnp.pi * INIT_IMAG * u2
        return {'x': jax.random.normal(ks[0], (B, T, D_IN), dtype=jnp.float32), 'W_in': _lecun(ks[1], (D_IN, D_HIDDEN), D_IN), 'b_in': jnp.zeros((D_HIDDEN,), jnp.float32), 'W_gx': _lecun(ks[2], (N_BLOCKS, blk_in, blk_out), blk_in), 'b_gx': _lecun(ks[3], (N_BLOCKS, blk_out), blk_in), 'W_ga': _lecun(ks[4], (N_BLOCKS, blk_in, blk_out), blk_in), 'b_ga': _lecun(ks[5], (N_BLOCKS, blk_out), blk_in), 'a_real': a_real, 'a_imag': a_imag, 'W_out': _lecun(ks[6], (D_HIDDEN, D_OUT), D_HIDDEN), 'b_out': jnp.zeros((D_OUT,), jnp.float32)}
    _L0_attn_in = _L0_attn_setup()

    def _L0_ffn_setup():
        import jax, jax.numpy as jnp
        import numpy as np
        B, S, DIM = (4, 64, 256)
        E, INTER = (32, 128)
        G, TOPK_G, TOPK = (8, 4, 6)
        ROUTE_SCALE = 2.5
        SHARED_INTER = 2 * INTER

        def _gate(xf, gate_w):
            scores = jax.nn.sigmoid(xf @ gate_w.T)
            gs = scores.reshape(-1, G, E // G)
            group_scores = gs.max(axis=-1)
            _, gidx = jax.lax.top_k(group_scores, TOPK_G)
            gmask = jnp.any(jnp.arange(G)[None, None, :] == gidx[:, :, None], axis=1)
            masked = jnp.where(gmask[:, :, None], gs, -jnp.inf).reshape(-1, E)
            _, idx = jax.lax.top_k(masked, TOPK)
            w = jnp.take_along_axis(scores, idx, axis=1)
            w = w / jnp.sum(w, axis=-1, keepdims=True) * ROUTE_SCALE
            return (w, idx)
        key = jax.random.key(seed)
        ks = jax.random.split(key, 8)
        sd = 0.02
        return {'x': jax.random.normal(ks[0], (B, S, DIM), jnp.float32), 'gate_w': jax.random.normal(ks[1], (E, DIM), jnp.float32) * sd, 'w11': jax.random.normal(ks[2], (E, INTER, DIM), jnp.float32) * sd, 'w33': jax.random.normal(ks[3], (E, INTER, DIM), jnp.float32) * sd, 'w22': jax.random.normal(ks[4], (E, DIM, INTER), jnp.float32) * sd, 'sw1': jax.random.normal(ks[5], (SHARED_INTER, DIM), jnp.float32) * sd, 'sw2': jax.random.normal(ks[6], (DIM, SHARED_INTER), jnp.float32) * sd, 'sw3': jax.random.normal(ks[7], (SHARED_INTER, DIM), jnp.float32) * sd}
    _L0_ffn_in = _L0_ffn_setup()
    _d = {'L0_attn_x': _L0_attn_in['x'], 'L0_attn_W_in': _L0_attn_in['W_in'], 'L0_attn_b_in': _L0_attn_in['b_in'], 'L0_attn_W_gx': _L0_attn_in['W_gx'], 'L0_attn_b_gx': _L0_attn_in['b_gx'], 'L0_attn_W_ga': _L0_attn_in['W_ga'], 'L0_attn_b_ga': _L0_attn_in['b_ga'], 'L0_attn_a_real': _L0_attn_in['a_real'], 'L0_attn_a_imag': _L0_attn_in['a_imag'], 'L0_attn_W_out': _L0_attn_in['W_out'], 'L0_attn_b_out': _L0_attn_in['b_out'], 'L0_ffn_gate_w': _L0_ffn_in['gate_w'], 'L0_ffn_w11': _L0_ffn_in['w11'], 'L0_ffn_w33': _L0_ffn_in['w33'], 'L0_ffn_w22': _L0_ffn_in['w22'], 'L0_ffn_sw1': _L0_ffn_in['sw1'], 'L0_ffn_sw2': _L0_ffn_in['sw2'], 'L0_ffn_sw3': _L0_ffn_in['sw3']}
    _x0 = _d['L0_attn_x']
    _d['L0_attn_x'] = jax.random.normal(jax.random.fold_in(jax.random.key(seed), 1), (4, 512, 256), dtype=_x0.dtype)
    del _x0
    return _d

def reference(L0_attn_x, L0_attn_W_in, L0_attn_b_in, L0_attn_W_gx, L0_attn_b_gx, L0_attn_W_ga, L0_attn_b_ga, L0_attn_a_real, L0_attn_a_imag, L0_attn_W_out, L0_attn_b_out, L0_ffn_gate_w, L0_ffn_w11, L0_ffn_w33, L0_ffn_w22, L0_ffn_sw1, L0_ffn_sw2, L0_ffn_sw3):

    def _L0_attn_ref(x, W_in, b_in, W_gx, b_gx, W_ga, b_ga, a_real, a_imag, W_out, b_out):
        import jax, jax.numpy as jnp
        import numpy as np
        B, T, D_IN = (8, 512, 256)
        D_HIDDEN = 256
        D_OUT = 256
        N_BLOCKS = 8
        R_MIN, R_MAX = (0.9, 0.999)
        INIT_IMAG = 0.1

        def _lecun(key, shape, fan_in):
            return (jax.random.normal(key, shape, dtype=jnp.float32) * np.sqrt(1.0 / fan_in)).astype(jnp.float32)

        def _block_diag_linear(x, W, b):
            h, i, j = W.shape
            xb = x.reshape(x.shape[0], x.shape[1], h, i)
            y = jnp.einsum('bthi,hij->bthj', xb, W) + b
            return y.reshape(y.shape[0], y.shape[1], h * j)

        def _linear_scan(a, x):

            def combine(l, r):
                al, bl = l
                ar, br = r
                return (al * ar, ar * bl + br)
            _, h = jax.lax.associative_scan(combine, (a, x), axis=1)
            return h

        def _reference_tuple_inner(x, W_in, b_in, W_gx, b_gx, W_ga, b_ga, a_real, a_imag, W_out, b_out):
            xh = x @ W_in + b_in
            gate_x = jax.nn.sigmoid(_block_diag_linear(xh, W_gx, b_gx))
            gate_a = jax.nn.sigmoid(_block_diag_linear(xh, W_ga, b_ga))
            log_a_re = -8.0 * gate_a * jax.nn.softplus(a_real)
            log_a_im = a_imag * gate_a
            a = jnp.exp(jax.lax.complex(log_a_re, log_a_im))
            a_sq = jnp.exp(jax.lax.complex(2.0 * log_a_re, 2.0 * log_a_im))
            xr, xi = jnp.split(xh, 2, axis=-1)
            xc = jax.lax.complex(xr, xi) * gate_x
            xc = jnp.sqrt(1.0 - a_sq) * xc
            h = _linear_scan(a, xc)
            h_m = jnp.concatenate([h.real, h.imag], axis=-1)
            out = h_m @ W_out + b_out
            h_last = h_m[:, -1]
            return (out, h_last)
        return _reference_tuple_inner(x, W_in, b_in, W_gx, b_gx, W_ga, b_ga, a_real, a_imag, W_out, b_out)[0]

    def _L0_ffn_ref(x, gate_w, w11, w33, w22, sw1, sw2, sw3):
        import jax, jax.numpy as jnp
        import numpy as np
        B, S, DIM = (4, 64, 256)
        E, INTER = (32, 128)
        G, TOPK_G, TOPK = (8, 4, 6)
        ROUTE_SCALE = 2.5
        SHARED_INTER = 2 * INTER

        def _gate(xf, gate_w):
            scores = jax.nn.sigmoid(xf @ gate_w.T)
            gs = scores.reshape(-1, G, E // G)
            group_scores = gs.max(axis=-1)
            _, gidx = jax.lax.top_k(group_scores, TOPK_G)
            gmask = jnp.any(jnp.arange(G)[None, None, :] == gidx[:, :, None], axis=1)
            masked = jnp.where(gmask[:, :, None], gs, -jnp.inf).reshape(-1, E)
            _, idx = jax.lax.top_k(masked, TOPK)
            w = jnp.take_along_axis(scores, idx, axis=1)
            w = w / jnp.sum(w, axis=-1, keepdims=True) * ROUTE_SCALE
            return (w, idx)
        xf = x.reshape(-1, DIM)
        T = xf.shape[0]
        w, idx = _gate(xf, gate_w)
        c = jnp.zeros((T, E), xf.dtype).at[jnp.arange(T)[:, None], idx].add(w)
        g = jnp.einsum('td,eid->tei', xf, w11)
        u = jnp.einsum('td,eid->tei', xf, w33)
        act = jax.nn.silu(g) * u
        y = jnp.einsum('tei,te,edi->td', act, c, w22)
        shared = jax.nn.silu(xf @ sw1.T) * (xf @ sw3.T) @ sw2.T
        return (y + shared).reshape(x.shape)
    x = L0_attn_x
    x = x + _L0_attn_ref(_layernorm(x, axis=-1), L0_attn_W_in, L0_attn_b_in, L0_attn_W_gx, L0_attn_b_gx, L0_attn_W_ga, L0_attn_b_ga, L0_attn_a_real, L0_attn_a_imag, L0_attn_W_out, L0_attn_b_out)
    x = x + _L0_ffn_ref(_layernorm(x, axis=-1), L0_ffn_gate_w, L0_ffn_w11, L0_ffn_w33, L0_ffn_w22, L0_ffn_sw1, L0_ffn_sw2, L0_ffn_sw3)
    return x

_drawn_inputs = setup_inputs


def setup_inputs(seed=0):
    import zlib

    import numpy as np

    out = dict(_drawn_inputs(seed))
    spreads = {'L0_attn_b_in': (0.0, 0.1), 'L0_attn_b_out': (0.0, 0.1)}
    factors = {'L0_ffn_gate_w': 6.17,
     'L0_ffn_w11': 5.616,
     'L0_ffn_w33': 5.533,
     'L0_ffn_w22': 5.537,
     'L0_ffn_sw1': 4.066,
     'L0_ffn_sw2': 4.069,
     'L0_ffn_sw3': 4.033}
    for name, (base, spread) in spreads.items():
        noise = np.random.default_rng([zlib.crc32(name.encode()), seed]).standard_normal(out[name].shape)
        drawn = base * np.exp(spread * noise) if base else spread * noise
        out[name] = jnp.asarray(drawn.astype(out[name].dtype))
    for name, factor in factors.items():
        out[name] = (out[name] * factor).astype(out[name].dtype)
    return out
```

```python
import concourse.bass as bass
from concourse import mybir
from concourse.alu_op_type import AluOpType as ALU
from contextlib import ExitStack
import math


def preln_recurrence_moe(nc, x, chan, w_in, w_gx, w_ga, w_out, b_out, gate_wt, experts, sw13, sw2, out):
    f32 = mybir.dt.float32
    bf16 = mybir.dt.bfloat16
    i32 = mybir.dt.int32
    u32 = mybir.dt.uint32
    ACT = mybir.ActivationFunctionType
    X = mybir.AxisListType.X

    B, SEQ, D = x.shape
    N = B * SEQ
    P = 128
    KD = D // P
    TS = SEQ // P
    NT = N // P
    E, GRP, TOPG, TOPK = 32, 8, 4, 6
    PER = E // GRP
    ROUTE_SCALE = 2.5
    EPS = 1e-5
    CAP = N + P
    PADROW = E * CAP
    ROW = D + 2
    BLOCKS = N * TOPK // P + E
    EW = KD * 2 * P + D
    NXS = 8
    NY = 4
    SKIP = 1 << 20
    MAGIC = 1.5 * 2.0 ** 23
    TWO_PI = 6.283185
    LN2H = 0.5 * math.log(2.0)

    xt_d = x.rearrange("b (t p) d -> b p t d", p=P)
    out_d = out.rearrange("b (t p) d -> (b t) p d", p=P)
    bucket = nc.dram_tensor("bucket_rows", (E * CAP + P, ROW), f32)
    choice = nc.dram_tensor("choice_rows", (N * TOPK, D), f32)
    bucket_ap = bucket.ap()
    choice_ap = choice.ap()
    choice_t = choice_ap.rearrange("(n p k) d -> n p (k d)", p=P, k=TOPK)

    ctx = ExitStack()
    with ctx:
        def sb(name, shape, dt=f32):
            return ctx.enter_context(nc.sbuf_tensor(name, shape, dt))

        def sem(name):
            return ctx.enter_context(nc.semaphore(name))

        W = sb("expert_weights", [P, E * EW])
        UNITS = 40
        EARLY = (E * EW - UNITS * SEQ) // EW
        base = E * EW - UNITS * SEQ

        def unit(u, k=1):
            return W[:, base + u * SEQ: base + (u + k) * SEQ]

        XH = [unit(0, 2), unit(2, 2)]
        SN = [unit(4, 2), unit(6, 2)]
        CS = [unit(8, 2), unit(10, 2)]
        GX = [unit(12), unit(13)]
        RHO = [unit(14), unit(15)]
        T = [unit(16 + i) for i in range(8)]
        XNT = unit(24, 2)
        FR = unit(26, 2)
        XN = unit(28, 2)
        AB = sb("turn_abs", [P, 2 * SEQ])
        GU = unit(30, 2)
        RHO2 = unit(32)
        E2 = unit(33)
        Q = unit(34)
        W1 = unit(35)
        ZR = unit(36)
        M2 = unit(37)
        SR = unit(38)
        RR = unit(39)

        resid = sb("resid", [P, NT, D])
        XN2T = sb("xn2_t", [P, B, KD, SEQ])
        PAY = sb("payload", [P, TS, TOPK, ROW])
        PADT = sb("pad_rows", [P, ROW])
        w_in_s = sb("w_in_s", [P, KD, D])
        w_out_s = sb("w_out_s", [P, KD, D])
        w_out_n = sb("w_out_n", [P, D])
        bd = sb("gate_blockdiag", [P, 2, KD, P])
        sw13_s = sb("sw13_s", [P, KD, 2, D])
        sw2_s = sb("sw2_s", [P, KD, D])
        gwt_s = sb("gwt_s", [P, KD, E])
        bout_s = sb("bout_s", [P, D])
        chan_s = sb("chan_s", [P, 6])
        ident = sb("ident", [P, P])
        tri = sb("tri", [P, P], bf16)
        ones = sb("ones", [P, P], bf16)
        iota_g = sb("iota_g", [P, GRP])
        iota_e = sb("iota_e", [P, E])
        iota_p = sb("iota_p", [P, 1])
        thr = sb("thr", [P, NT])
        cb0 = sb("bucket_base", [P, E])
        cb = sb("bucket_next", [P, E])
        cst = sb("consts", [P, 4])
        ch = sb("chan_derived", [P, 10])
        st1 = sb("st1", [P, TS, 6])
        mv1 = sb("mv1", [P, TS, 2])
        rs1 = sb("rs1", [P, 2, TS])
        mv2 = sb("mv2", [P, TS, 2])
        rs2 = sb("rs2", [P, 2, TS])
        sc = sb("scores", [P, TS, E])
        sc2 = sb("scores_tmp", [P, 2, TS, E])
        gm = sb("group_max", [P, TS, GRP])
        gv = sb("gv", [P, TS, 8])
        gi = sb("gi", [P, TS, 8], u32)
        gif = sb("gif", [P, TS, TOPG])
        geq = sb("geq", [P, TS, GRP, TOPG])
        gmask = sb("gmask", [P, TS, GRP])
        gmm = sb("gmm", [P, TS, GRP])
        msk = sb("masked", [P, TS, E])
        ev = sb("ev", [P, TS, 8])
        ei = sb("ei", [P, TS, 8], u32)
        eif = sb("eif", [P, TS, TOPK])
        wsum = sb("wsum", [P, 2, TS])
        oh = sb("one_hot", [P, TS * TOPK, E])
        memb = sb("member", [P, TS, E], bf16)
        dpos = sb("dpos", [P, TS, E])
        dest = sb("dest", [P, 2, TS * TOPK], i32)
        destf = sb("destf", [P, TS * TOPK])
        cnt = sb("cnt", [P, 6, E])
        zero_e = sb("zero_e", [P, E])
        cmpb = sb("cmpb", [P, E, NT])
        tabf = sb("tabf", [P, 4])
        tabs = sb("tabs", [1, 2 * P + E], i32)
        xs = sb("xs", [P, NXS, ROW])
        xT = sb("xT", [P, 2, D])
        sg = sb("sg", [P, 2, P])
        hh = sb("hh", [P, 2, P])
        hT = sb("hT", [P, 2, P])
        yy = sb("yy", [P, 4, D])
        xs_idx = xs[:, :, :].bitcast(i32)
        SHG = AB

        PS = ctx.enter_context(nc.psum_tensor("PS", [P, 8, 512], f32))

        s_x = [sem(f"x_loaded{b}") for b in range(B)]
        s_small = sem("small_weights_loaded")
        s_gatew = sem("gate_weights_loaded")
        s_shw = sem("shared_weights_loaded")
        s_wearly = sem("early_experts_loaded")
        s_wlate = sem("late_experts_loaded")
        s_const = sem("constants_built")
        s_bdz = sem("blockdiag_zeroed")
        s_bout = sem("output_bias_added")
        s_dve = sem("dve_chain")
        s_act = sem("act_chain")
        s_pool = sem("pool_chain")
        s_spin = sem("softplus_input")
        s_spout = sem("softplus_log")
        s_chan = sem("channel_constants")
        s_stats1 = sem("ln1_stats")
        s_rstd1 = sem("ln1_rstd")
        s_xn = sem("ln1_rows")
        s_xntp = sem("ln1_transposed_psum")
        s_xnt = sem("ln1_transposed")
        s_xhp = sem("projected_psum")
        s_xh = sem("projected")
        s_gp = sem("gates_psum")
        s_gates = sem("gates")
        s_rho = sem("decay_ready")
        s_turn = sem("turns_reduced")
        s_trig = sem("sines_ready")
        s_m2 = sem("z_squared_abs")
        s_zabs = sem("z_abs_ready")
        s_zt = sem("z_abs_plus_re")
        s_zroot = sem("z_root_ready")
        s_xused = sem("projection_used")
        s_prod = sem("rotated_products")
        s_outp = sem("attention_out_psum")
        s_x1 = sem("first_residual")
        s_stats2 = sem("ln2_stats")
        s_rstd2 = sem("ln2_rstd")
        s_pay = sem("ln2_rows")
        s_xn2p = sem("ln2_transposed_psum")
        s_xn2 = sem("ln2_transposed")
        s_lgp = sem("router_logits_psum")
        s_sc = sem("router_scores")
        s_memb = sem("membership")
        s_posp = sem("positions_psum")
        s_dest = sem("bucket_rows_known")
        s_rowid = sem("output_row_ids")
        s_scat = [sem(f"rows_scattered{b}") for b in range(B)]
        s_tabf = sem("block_table_columns")
        s_tabp = sem("block_table_psum")
        s_tab = sem("block_table")
        s_padt = sem("padding_tile")
        s_pad = sem("padding_written")
        s_shgp = sem("shared_gate_up_psum")
        s_shs = sem("shared_silu")
        s_shh = sem("shared_hidden")
        s_shyp = sem("shared_out_psum")
        s_resid = sem("second_residual")
        s_xs = [sem(f"block_rows{i}") for i in range(NXS)]
        s_xtp = sem("block_transposed_psum")
        s_xt = sem("block_transposed")
        s_gup = sem("block_gate_up_psum")
        s_sg = sem("block_silu")
        s_hh = sem("block_hidden")
        s_hp = sem("hidden_transposed_psum")
        s_ht = sem("hidden_transposed")
        s_yp = sem("block_out_psum")
        s_y = sem("block_out")
        s_ys = [sem(f"block_scattered{i}") for i in range(NY)]
        s_cin = [sem(f"choices_loaded{i}") for i in range(4)]
        s_fin = sem("token_summed")
        s_out = [sem(f"token_stored{i}") for i in range(4)]

        block = ctx.enter_context(nc.Block())

        class Chain:

            def __init__(self, eng, s):
                self.eng, self.s, self.n = eng, s, 0

            def add(self, ins):
                ins.then_inc(self.s, 1)
                self.n += 1

            def wait(self):
                self.eng.wait_ge(self.s, self.n)

        def at_least(eng, s, n):
            if n > 0:
                eng.wait_ge(s, n)

        def tiles(b):
            return slice(b * TS, (b + 1) * TS)

        @block.sync
        def _(sp):
            for b in range(B):
                sp.dma_start(resid[:, tiles(b), :], xt_d[b]).then_inc(s_x[b], 16)
                if b == 0:
                    sp.dma_start(w_in_s[:], w_in.rearrange("(k p) n -> p k n", p=P)).then_inc(s_small, 16)
                    sp.dma_start(chan_s[:], chan).then_inc(s_small, 16)
                    sp.dma_start(bout_s[:], b_out.partition_broadcast(P)).then_inc(s_small, 16)
                    sp.dma_start(gwt_s[:], gate_wt).then_inc(s_small, 16)
                    sp.dma_start(w_out_s[:], w_out.rearrange("(k p) n -> p k n", p=P)).then_inc(s_small, 16)
            sp.dma_start(sw13_s[:], sw13).then_inc(s_shw, 16)
            sp.dma_start(sw2_s[:], sw2).then_inc(s_shw, 16)
            sp.dma_start(W[:, 0:EARLY * EW].rearrange("p (e w) -> p e w", w=EW), experts[:, 0:EARLY, :]).then_inc(s_wearly, 16)
            sp.wait_ge(s_padt, 3)
            sp.dma_start(bucket_ap[PADROW:PADROW + P, :], PADT[:]).then_inc(s_pad, 16)
            sp.wait_ge(s_outp, B)
            sp.wait_ge(s_prod, B)
            sp.wait_ge(s_zroot, B)
            sp.dma_start(W[:, EARLY * EW:].rearrange("p (e w) -> p e w", w=EW), experts[:, EARLY:, :]).then_inc(s_wlate, 16)
            sp.wait_ge(s_tab, 1)
            for e in range(E):
                row = sp.value_load(tabs[0:1, 2 * P + e:2 * P + e + 1], min_val=0, max_val=E * CAP)
                sp.dma_start(bucket_ap[bass.ds(row, P), :], PADT[:]).then_inc(s_pad, 16)
            sp.wait_ge(s_pad, 16 * (E + 1))
            for b in range(B):
                sp.wait_ge(s_scat[b], 16 * TS * TOPK)

            def load_block(j, slot, tail_rounds):
                if tail_rounds is not None:
                    sp.wait_ge(s_ys[slot % NY], tail_rounds)
                row = sp.value_load(tabs[0:1, bass.ds(j, 1)], min_val=0, max_val=E * CAP)
                sp.dma_start(xs[:, slot, :], bucket_ap[bass.ds(row, P), :]).then_inc(s_xs[slot], 16)

            for j in range(NXS):
                load_block(j, j, None)
            with sp.Fori(NXS, BLOCKS, NXS) as i:
                for u in range(NXS):
                    load_block(i + u, u, (i - NXS) * (16 // NY) + 16 * (u // NY + 1))
            for q in range(NY):
                sp.wait_ge(s_ys[q], 16 * (BLOCKS // NY))
            cmb = PAY[:, :, :, :].rearrange("p t k r -> p (t k r)")
            for n in range(NT):
                if n >= 4:
                    sp.wait_ge(s_fin, n - 3)
                sp.dma_start(cmb[:, (n % 4) * TOPK * D:(n % 4 + 1) * TOPK * D], choice_t[n]).then_inc(s_cin[n % 4], 16)

        @block.gpsimd
        def _(pool):
            pch = Chain(pool, s_pool)
            pch.add(nc.gpsimd.memset(ident[:], 0.0))
            pch.add(nc.gpsimd.memset(tri[:], 1.0))
            nc.gpsimd.memset(bd[:], 0.0).then_inc(s_bdz, 1)
            pch.wait()
            nc.gpsimd.affine_select(out=ident[:], in_=ident[:], compare_op=ALU.not_equal, fill=1.0, base=0,
                                    pattern=[[-1, P]], channel_multiplier=1).then_inc(s_const, 1)
            pool.wait_ge(s_bdz, 1)
            HB, GI, GO = w_gx.shape
            for g, w in enumerate((w_gx, w_ga)):
                for h in range(HB):
                    k, r = divmod(h * GI, P)
                    pool.dma_start(bd[r:r + GI, g, k, h * GO:(h + 1) * GO], w[h]).then_inc(s_gatew, 16)
            nc.gpsimd.affine_select(out=tri[:], in_=tri[:], compare_op=ALU.is_gt, fill=0.0, base=0,
                                    pattern=[[1, P]], channel_multiplier=-1).then_inc(s_const, 1)
            nc.gpsimd.memset(ones[:], 1.0).then_inc(s_const, 1)
            nc.gpsimd.iota(iota_g[:], pattern=[[1, GRP]], base=0, channel_multiplier=0,
                           allow_small_or_imprecise_dtypes=True).then_inc(s_const, 1)
            nc.gpsimd.iota(iota_e[:], pattern=[[1, E]], base=0, channel_multiplier=0,
                           allow_small_or_imprecise_dtypes=True).then_inc(s_const, 1)
            nc.gpsimd.iota(iota_p[:], pattern=[[0, 1]], base=0, channel_multiplier=1,
                           allow_small_or_imprecise_dtypes=True).then_inc(s_const, 1)
            nc.gpsimd.iota(thr[:], pattern=[[P, NT]], base=0, channel_multiplier=0,
                           allow_small_or_imprecise_dtypes=True).then_inc(s_const, 1)
            nc.gpsimd.iota(cb0[:], pattern=[[CAP, E]], base=0, channel_multiplier=0,
                           allow_small_or_imprecise_dtypes=True).then_inc(s_const, 1)
            nc.gpsimd.memset(zero_e[:], 0.0).then_inc(s_const, 1)
            nc.gpsimd.memset(PADT[:, 0:D], 0.0).then_inc(s_padt, 1)
            nc.gpsimd.memset(PADT[:, D + 1:D + 2], 0.0).then_inc(s_padt, 1)
            nc.gpsimd.iota(PADT[:, D:D + 1].bitcast(i32), pattern=[[0, 1]], base=SKIP,
                           channel_multiplier=0).then_inc(s_padt, 1)
            pool.wait_ge(s_small, 80)
            pay_idx = PAY[:, :, :, :].bitcast(i32)
            for b in range(B):
                pool.wait_ge(s_xn, b + 1)
                nc.gpsimd.tensor_tensor(resid[:, tiles(b), :], resid[:, tiles(b), :],
                                        bout_s[:].unsqueeze(1).to_broadcast([P, TS, D]), ALU.add).then_inc(s_bout, 1)
            for b in range(B):
                if b >= 1:
                    pool.wait_ge(s_scat[b - 1], 16 * TS * TOPK)
                nc.gpsimd.iota(pay_idx[:, :, :, D], pattern=[[P * TOPK, TS], [1, TOPK]], base=b * SEQ * TOPK,
                               channel_multiplier=TOPK).then_inc(s_rowid, 1)
                pool.wait_ge(s_rowid, b + 1)
                pool.wait_ge(s_dest, b + 1)
                for t in range(TS):
                    for k in range(TOPK):
                        q = t * TOPK + k
                        nc.gpsimd.indirect_dma_start(
                            out=bucket_ap[:, :], out_offset=bass.IndirectOffsetOnAxis(ap=dest[:, b % 2, q:q + 1], axis=0),
                            in_=PAY[:, t, k, :], in_offset=None).then_inc(s_scat[b], 16)

            zero, last, last_row = (pool.alloc_register(n) for n in ("row_zero", "row_last", "row_bound"))
            pool.reg_mov(zero, 0)
            pool.reg_mov(last, N * TOPK - 1)

            def scatter(j, slot, ready):
                pool.wait_ge(s_y, ready)
                pool.reg_add(last_row, zero, last)
                nc.gpsimd.indirect_dma_start(
                    out=choice_ap[:, :], out_offset=bass.IndirectOffsetOnAxis(ap=xs_idx[:, slot, D:D + 1], axis=0),
                    in_=yy[:, slot % NY, :], in_offset=None,
                    bounds_check=last_row, oob_is_err=False).then_inc(s_ys[slot % NY], 16)

            with pool.Fori(0, BLOCKS, NXS) as i:
                for u in range(NXS):
                    scatter(i + u, u, i + u + 1)

        @block.scalar
        def _(act):
            ach = Chain(act, s_act)
            A = nc.scalar.activation

            def rstd(mv, rs, s_in, s_out, b):
                act.wait_ge(s_in, b + 1)
                ach.add(A(rs[:, 0, :], mv[:, :, 1], ACT.Ln, bias=cst[:, 2:3]))
                ach.wait()
                A(rs[:, 1, :], rs[:, 0, :], ACT.Exp, scale=-0.5).then_inc(s_out, 1)

            def project(b):
                p = b % 2
                act.wait_ge(s_xntp, b + 1)
                at_least(act, s_xhp, b)
                A(XNT, PS[:, 0:2, :], ACT.Copy).then_inc(s_xnt, 1)
                act.wait_ge(s_xhp, b + 1)
                at_least(act, s_xused, b - 1)
                for k in range(KD):
                    A(XH[p][:, k * SEQ:(k + 1) * SEQ], PS[:, 2 + k, :], ACT.Identity,
                      bias=chan_s[:, k:k + 1]).then_inc(s_xh, 1)

            def decay(b):
                p = b % 2
                act.wait_ge(s_gp, b + 1)
                A(GX[p], PS[:, 4, :], ACT.Sigmoid, bias=chan_s[:, 2:3]).then_inc(s_gates, 1)
                at_least(act, s_turn, b)
                A(GU[:, 0:SEQ], PS[:, 5, :], ACT.Sigmoid, bias=chan_s[:, 3:4]).then_inc(s_gates, 1)
                act.wait_ge(s_gates, 2 * b + 2)
                at_least(act, s_prod, b - 1)
                at_least(act, s_m2, b)
                if b == 0:
                    act.wait_ge(s_chan, 1)
                A(RHO[p], GU[:, 0:SEQ], ACT.Exp, scale=ch[:, 1:2]).then_inc(s_rho, 1)
                ach.add(A(RHO2, GU[:, 0:SEQ], ACT.Exp, scale=ch[:, 2:3]))
                ach.wait()
                A(E2, RHO2, ACT.Square, scale=-1.0, bias=1.0).then_inc(s_rho, 1)

            def sines(b):
                p = b % 2
                act.wait_ge(s_turn, b + 1)
                A(SN[p], FR, ACT.Sin, scale=TWO_PI)
                A(CS[p], AB[:], ACT.Sin, scale=-TWO_PI, bias=cst[:, 0:1]).then_inc(s_trig, 1)

            def zabs(b):
                act.wait_ge(s_m2, b + 1)
                ach.add(A(M2, M2, ACT.Ln, bias=cst[:, 1:2]))
                ach.wait()
                A(M2, M2, ACT.Exp, scale=0.5).then_inc(s_zabs, 1)

            def zroots(b):
                act.wait_ge(s_zt, b + 1)
                ach.add(A(M2, M2, ACT.Ln))
                ach.wait()
                A(SR, M2, ACT.Exp, scale=0.5, bias=cst[:, 3:4])
                A(RR, M2, ACT.Exp, scale=-0.5, bias=cst[:, 3:4]).then_inc(s_zroot, 1)

            def ln2_transposed(b):
                act.wait_ge(s_xn2p, b + 1)
                A(XN2T[:, b, :, :], PS[:, 0:2, :], ACT.Copy).then_inc(s_xn2, 1)

            def scores(b):
                act.wait_ge(s_lgp, b + 1)
                at_least(act, s_memb, b)
                ach.add(A(sc2[:, 0, :, :], PS[:, 2, 0:TS * E].rearrange("p (t e) -> p t e", e=E), ACT.Exp, scale=-1.0))
                ach.wait()
                ach.add(A(sc2[:, 1, :, :], sc2[:, 0, :, :], ACT.Ln, bias=1.0))
                ach.wait()
                A(sc[:, :, :], sc2[:, 1, :, :], ACT.Exp, scale=-1.0).then_inc(s_sc, 1)

            act.wait_ge(s_spin, 1)
            ach.add(A(ch[:, 4:5], ch[:, 3:4], ACT.Exp, scale=-1.0))
            ach.wait()
            A(ch[:, 5:6], ch[:, 4:5], ACT.Ln, bias=1.0).then_inc(s_spout, 1)
            rstd(mv1, rs1, s_stats1, s_rstd1, 0)
            project(0)
            rstd(mv1, rs1, s_stats1, s_rstd1, 1)
            decay(0)
            sines(0)
            zabs(0)
            zroots(0)
            for b in range(B + 1):
                if b + 1 < B:
                    project(b + 1)
                    decay(b + 1)
                if b >= 1:
                    rstd(mv2, rs2, s_stats2, s_rstd2, b - 1)
                if b + 1 < B:
                    sines(b + 1)
                if b >= 1:
                    ln2_transposed(b - 1)
                    scores(b - 1)
                if b + 1 < B:
                    zabs(b + 1)
                if b + 2 < B:
                    rstd(mv1, rs1, s_stats1, s_rstd1, b + 2)
                if b + 1 < B:
                    zroots(b + 1)

            def shared(b):
                act.wait_ge(s_shgp, b + 1)
                at_least(act, s_shyp, b)
                A(SHG[:].rearrange("p (h n) -> p h n", h=KD), PS[:, 2:4, :], ACT.Silu).then_inc(s_shs, 1)

            def silu(j, r):
                act.wait_ge(s_gup, j + 1)
                if not isinstance(j, int) or j >= 2:
                    act.wait_ge(s_hh, j - 1)
                A(sg[:, r, :], PS[:, 2 + r, 0:P], ACT.Silu).then_inc(s_sg, 1)

            def hidden_t(j, r):
                act.wait_ge(s_hp, j + 1)
                if not isinstance(j, int) or j >= 2:
                    act.wait_ge(s_yp, j - 1)
                A(hT[:, r, :], PS[:, 4 + r, 0:P], ACT.Copy).then_inc(s_ht, 1)

            def rows_t(j, r):
                act.wait_ge(s_xtp, j + 1)
                if not isinstance(j, int) or j >= 2:
                    act.wait_ge(s_gup, j - 1)
                A(xT[:, r, :], PS[:, r, 0:D], ACT.Copy).then_inc(s_xt, 1)

            for b in range(2):
                shared(b)

            def step(s, u):
                if not isinstance(s, int) or 1 <= s <= BLOCKS:
                    silu(s - 1, (u - 1) % 2)
                if not isinstance(s, int) or 2 <= s <= BLOCKS + 1:
                    hidden_t(s - 2, u % 2)
                if not isinstance(s, int) or s < BLOCKS:
                    rows_t(s, u % 2)

            for s in range(NXS):
                step(s, s)
            with act.Fori(NXS, BLOCKS, NXS) as i:
                for u in range(NXS):
                    step(i + u, u)
            for s in range(BLOCKS, BLOCKS + 3):
                step(s, s)
            for b in range(2, B):
                shared(b)
            for n in range(NT):
                act.wait_ge(s_fin, n + 1)
                act.dma_start(out_d[n], resid[:, n, :]).then_inc(s_out[n % 4], 16)
            for q in range(4):
                act.wait_ge(s_out[q], 16 * (NT // 4))

        @block.vector
        def _(dve):
            c = Chain(dve, s_dve)
            V = nc.vector
            TT, TSC, STT = V.tensor_tensor, V.tensor_scalar, V.scalar_tensor_tensor
            M, AD, SU = ALU.mult, ALU.add, ALU.subtract

            def stats(src, b, st, mv, s_out):
                for t in range(TS):
                    c.add(V.bn_stats(st[:, t, :], src[:, b * TS + t, :]))
                c.wait()
                for t in range(TS):
                    ins = V.bn_aggr(mv[:, t, :], st[:, t, :])
                ins.then_inc(s_out, 1)

            def ln1_rows(b):
                dve.wait_ge(s_rstd1, b + 1)
                at_least(dve, s_xntp, b)
                for t in range(TS):
                    ins = TSC(XN[:, t * D:(t + 1) * D], resid[:, b * TS + t, :], mv1[:, t, 0:1], rs1[:, 1, t:t + 1], SU, M)
                ins.then_inc(s_xn, 1)

            def turns(b):
                dve.wait_ge(s_gates, 2 * b + 2)
                at_least(dve, s_trig, b)
                c.add(V.tensor_tensor_scan(GU[:, SEQ:], GU[:, 0:SEQ], GU[:, 0:SEQ], 0.0, AD, ALU.bypass))
                c.wait()
                c.add(TSC(AB[:], GU, ch[:, 0:1], MAGIC, M, AD))
                c.wait()
                c.add(TSC(AB[:], AB[:], MAGIC, None, SU))
                c.wait()
                c.add(STT(FR, GU, ch[:, 0:1], AB[:], M, SU))
                c.wait()
                TSC(AB[:].bitcast(i32), FR.bitcast(i32), 0x7FFFFFFF, None, ALU.bitwise_and).then_inc(s_turn, 1)

            def z_parts(b):
                p = b % 2
                s, co = SN[p][:, 0:SEQ], CS[p][:, 0:SEQ]
                dve.wait_ge(s_trig, b + 1)
                dve.wait_ge(s_rho, 2 * b + 2)
                c.add(STT(Q, s, 2.0, RHO2, M, M))
                c.wait()
                c.add(TT(W1, Q, s, M))
                c.add(TT(Q, Q, co, M))
                dve.wait_ge(s_dve, c.n - 1)
                c.add(STT(ZR, W1, 1.0, RHO2, AD, SU))
                STT(M2, W1, 2.0, E2, M, AD).then_inc(s_m2, 1)

            def z_sum(b):
                dve.wait_ge(s_zabs, b + 1)
                c.wait()
                c.add(TT(M2, M2, ZR, AD))
                c.wait()
                TSC(M2, M2, 1e-30, None, ALU.max).then_inc(s_zt, 1)

            def gate_input(b):
                p = b % 2
                dve.wait_ge(s_zroot, b + 1)
                dve.wait_ge(s_xh, 2 * b + 2)
                at_least(dve, s_outp, b)
                c.add(TT(Q, Q, RR, M))
                c.add(TT(T[0], XH[p][:, 0:SEQ], GX[p], M))
                ins = TT(T[1], XH[p][:, SEQ:], GX[p], M)
                ins.then_inc(s_xused, 1)
                c.wait()
                c.add(TT(T[2], T[0], SR, M))
                c.add(TT(T[5], T[0], Q, M))
                dve.wait_ge(s_xused, b + 1)
                c.add(TT(T[3], T[1], Q, M))
                c.add(TT(T[4], T[1], SR, M))
                dve.wait_ge(s_dve, c.n - 1)
                c.add(TT(T[2], T[2], T[3], AD))
                dve.wait_ge(s_dve, c.n - 1)
                c.add(TT(T[4], T[4], T[5], SU))

            def rotate_back(b):
                p = b % 2
                s, co = SN[p][:, SEQ:], CS[p][:, SEQ:]
                c.wait()
                c.add(TT(T[0], T[2], co, M))
                c.add(TT(T[1], T[4], s, M))
                c.add(TT(T[3], T[4], co, M))
                c.add(TT(T[5], T[2], s, M))
                dve.wait_ge(s_dve, c.n - 2)
                c.add(TT(T[0], T[0], T[1], AD))
                dve.wait_ge(s_dve, c.n - 1)
                c.add(TT(T[3], T[3], T[5], SU))

            def scan_rotate(b):
                p = b % 2
                s, co = SN[p][:, SEQ:], CS[p][:, SEQ:]
                c.wait()
                c.add(V.tensor_tensor_scan(T[6], RHO[p], T[0], 0.0, M, AD))
                c.add(V.tensor_tensor_scan(T[7], RHO[p], T[3], 0.0, M, AD))
                dve.wait_ge(s_dve, c.n - 1)
                TT(T[1], T[6], co, M)
                TT(T[4], T[6], s, M)
                c.wait()
                TT(T[2], T[7], s, M)
                TT(T[5], T[7], co, M).then_inc(s_prod, 1)

            def residual1(b):
                dve.wait_ge(s_outp, b + 1)
                dve.wait_ge(s_bout, b + 1)
                TT(resid[:, tiles(b), :], resid[:, tiles(b), :],
                   PS[:, 6:8, :].rearrange("p a (c d) -> p (a c) d", d=D), AD).then_inc(s_x1, 1)
                dve.wait_ge(s_x1, b + 1)
                stats(resid, b, st1, mv2, s_stats2)

            def ln2_rows(b):
                dve.wait_ge(s_rstd2, b + 1)
                if b >= 1:
                    dve.wait_ge(s_scat[b - 1], 16 * TS * TOPK)
                for t in range(TS):
                    ins = TSC(PAY[:, t, :, 0:D], resid[:, b * TS + t, :].unsqueeze(1).to_broadcast([P, TOPK, D]),
                              mv2[:, t, 0:1], rs2[:, 1, t:t + 1], SU, M)
                ins.then_inc(s_pay, 1)

            def choose(b):
                dve.wait_ge(s_sc, b + 1)
                c.add(V.tensor_reduce(gm[:], sc[:, :, :].rearrange("p t (g m) -> p t g m", m=PER), X, ALU.max))
                c.wait()
                for t in range(TS):
                    c.add(V.max(gv[:, t, :], gm[:, t, :]))
                c.wait()
                for t in range(TS):
                    c.add(V.max_index(gi[:, t, :], gv[:, t, :], gm[:, t, :]))
                c.wait()
                c.add(V.tensor_copy(gif[:], gi[:, :, 0:TOPG]))
                c.wait()
                for t in range(TS):
                    c.add(TT(geq[:, t, :, :], iota_g[:].unsqueeze(2).to_broadcast([P, GRP, TOPG]),
                             gif[:, t, :].unsqueeze(1).to_broadcast([P, GRP, TOPG]), ALU.is_equal))
                c.wait()
                c.add(V.tensor_reduce(gmask[:], geq[:], X, ALU.max))
                c.wait()
                c.add(TSC(gmm[:], gmask[:], 1.0, None, SU))
                tg = TS * GRP
                c.add(TT(msk[:].rearrange("p t (g m) -> p (t g) m", m=PER), sc[:].rearrange("p t (g m) -> p (t g) m", m=PER),
                         gmask[:].rearrange("p t g -> p (t g)").unsqueeze(2).to_broadcast([P, tg, PER]), M))
                c.wait()
                c.add(TT(msk[:].rearrange("p t (g m) -> p (t g) m", m=PER), msk[:].rearrange("p t (g m) -> p (t g) m", m=PER),
                         gmm[:].rearrange("p t g -> p (t g)").unsqueeze(2).to_broadcast([P, tg, PER]), AD))
                c.wait()
                for t in range(TS):
                    c.add(V.max(ev[:, t, :], msk[:, t, :]))
                c.wait()
                for t in range(TS):
                    c.add(V.max_index(ei[:, t, :], ev[:, t, :], msk[:, t, :]))
                c.add(V.tensor_reduce(wsum[:, 0, :], ev[:, :, 0:TOPK], X, AD))
                c.wait()
                c.add(V.tensor_copy(eif[:], ei[:, :, 0:TOPK]))
                c.add(V.reciprocal(wsum[:, 1, :], wsum[:, 0, :]))
                dve.wait_ge(s_dve, c.n - 1)
                c.add(TT(oh[:], iota_e[:].unsqueeze(1).to_broadcast([P, TS * TOPK, E]),
                         eif[:].rearrange("p t k -> p (t k)").unsqueeze(2).to_broadcast([P, TS * TOPK, E]), ALU.is_equal))
                c.wait()
                V.tensor_reduce(memb[:], oh[:].rearrange("p (t k) e -> p t e k", k=TOPK), X, ALU.max).then_inc(s_memb, 1)
                c.add(STT(PAY[:, :, :, D + 1], ev[:, :, 0:TOPK], ROUTE_SCALE,
                          wsum[:, 1, :].unsqueeze(2).to_broadcast([P, TS, TOPK]), M, M))

            def places(b):
                dve.wait_ge(s_posp, b + 1)
                if b == 0:
                    c.add(V.tensor_copy(cb[:], cb0[:]))
                c.wait()
                c.add(TT(dpos[:], PS[:, 3, 0:TS * E].rearrange("p (t e) -> p t e", e=E),
                         cb[:].unsqueeze(1).to_broadcast([P, TS, E]), AD))
                c.wait()
                c.add(TT(cb[:], cb[:], PS[:, 3, TS * E:TS * E + E], AD))
                for t in range(TS):
                    c.add(TT(oh[:, t * TOPK:(t + 1) * TOPK, :], oh[:, t * TOPK:(t + 1) * TOPK, :],
                             dpos[:, t, :].unsqueeze(1).to_broadcast([P, TOPK, E]), M))
                c.wait()
                c.add(V.tensor_reduce(destf[:], oh[:], X, AD))
                c.wait()
                V.tensor_copy(dest[:, b % 2, :], destf[:]).then_inc(s_dest, 1)

            dve.wait_ge(s_small, 80)
            dve.wait_ge(s_const, 9)
            V.memset(cst[:, 0:1], math.pi / 2)
            V.memset(cst[:, 1:2], 1e-37)
            V.memset(cst[:, 2:3], EPS)
            V.memset(cst[:, 3:4], -LN2H)
            TSC(ch[:, 3:4].bitcast(i32), chan_s[:, 4:5].bitcast(i32), 0x7FFFFFFF, None, ALU.bitwise_and).then_inc(s_spin, 1)
            TSC(ch[:, 0:1], chan_s[:, 5:6], 1.0 / (2 * math.pi), None, M)
            c.add(TSC(ch[:, 7:8], chan_s[:, 4:5], 0.0, None, ALU.max))
            dve.wait_ge(s_x[0], 16)
            stats(resid, 0, st1, mv1, s_stats1)
            dve.wait_ge(s_spout, 1)
            c.add(TT(ch[:, 6:7], ch[:, 7:8], ch[:, 5:6], AD))
            c.wait()
            TSC(ch[:, 1:2], ch[:, 6:7], -8.0, None, M)
            TSC(ch[:, 2:3], ch[:, 6:7], -16.0, None, M).then_inc(s_chan, 1)
            ln1_rows(0)
            TSC(w_out_n[:], w_out_s[:, 0, :], -1.0, None, M).then_inc(s_chan, 1)
            dve.wait_ge(s_x[1], 16)
            stats(resid, 1, st1, mv1, s_stats1)
            ln1_rows(1)
            turns(0)
            z_parts(0)
            z_sum(0)
            for b in range(B + 1):
                if b < B:
                    gate_input(b)
                if b >= 1:
                    residual1(b - 1)
                if b + 1 < B:
                    turns(b + 1)
                if b < B:
                    rotate_back(b)
                if b >= 1:
                    ln2_rows(b - 1)
                if b + 1 < B:
                    z_parts(b + 1)
                if b < B:
                    scan_rotate(b)
                if b + 2 < B:
                    dve.wait_ge(s_x[b + 2], 16)
                    stats(resid, b + 2, st1, mv1, s_stats1)
                if b >= 1:
                    choose(b - 1)
                if b + 1 < B:
                    z_sum(b + 1)
                if b + 2 < B:
                    ln1_rows(b + 2)
                if b >= 1:
                    places(b - 1)

            CN, CBK, CUM, LE, TMP = 0, 1, 2, 3, 4
            c.add(TT(cnt[:, CN, :], cb[:], cb0[:], SU))
            c.wait()
            c.add(TT(cmpb[:], cnt[:, CN, :].unsqueeze(2).to_broadcast([P, E, NT]),
                     thr[:].unsqueeze(1).to_broadcast([P, E, NT]), ALU.is_gt))
            c.wait()
            c.add(V.tensor_reduce(cnt[:, CBK, :], cmpb[:], X, AD))
            c.wait()
            c.add(V.tensor_tensor_scan(cnt[:, CUM, :], cnt[:, CBK, :], zero_e[:], 0.0, AD, AD))
            c.wait()
            c.add(TSC(cnt[:, LE, :], cnt[:, CUM, :], iota_p[:, 0:1], None, ALU.is_le))
            c.wait()
            c.add(TT(cnt[:, TMP, :], cnt[:, LE, :], cnt[:, CBK, :], M))
            c.add(V.tensor_reduce(tabf[:, 0:1], cnt[:, LE, :], X, AD))
            c.wait()
            c.add(V.tensor_reduce(tabf[:, 1:2], cnt[:, TMP, :], X, AD))
            c.wait()
            c.add(TT(tabf[:, 1:2], iota_p[:], tabf[:, 1:2], SU))
            c.wait()
            c.add(TSC(tabf[:, 1:2], tabf[:, 1:2], float(P), None, M))
            c.wait()
            c.add(STT(tabf[:, 2:3], tabf[:, 0:1], float(CAP), tabf[:, 1:2], M, AD))
            c.wait()
            c.add(TSC(tabf[:, 2:3], tabf[:, 2:3], float(PADROW), None, ALU.min))
            c.add(TSC(tabf[:, 3:4], tabf[:, 0:1], float(E - 1), float(EW), ALU.min, M))
            c.wait()
            V.tensor_copy(tabs[0:1, 2 * P:2 * P + E], cb[0:1, :]).then_inc(s_tabf, 1)
            dve.wait_ge(s_tabp, 1)
            V.tensor_copy(tabs[0:1, 0:2 * P], PS[0:1, 0, 0:2 * P]).then_inc(s_tab, 1)

            def shared(b):
                dve.wait_ge(s_shs, b + 1)
                TT(SHG[:].rearrange("p (h n) -> p h n", h=KD), SHG[:].rearrange("p (h n) -> p h n", h=KD),
                   PS[:, 4:6, :], M).then_inc(s_shh, 1)
                dve.wait_ge(s_shyp, b + 1)
                TT(resid[:, tiles(b), :], resid[:, tiles(b), :],
                   PS[:, 6:8, :].rearrange("p a (c d) -> p (a c) d", d=D), AD).then_inc(s_resid, 1)

            for b in range(2):
                shared(b)

            def hidden(j, r, slot):
                dve.wait_ge(s_sg, j + 1)
                if not isinstance(j, int) or j >= 2:
                    dve.wait_ge(s_hp, j - 1)
                STT(hh[:, r, :], sg[:, r, :], xs[:, slot, D + 1:D + 2], PS[:, 2 + r, P:2 * P], M, M).then_inc(s_hh, 1)

            def block_out(j, r, slot, scattered):
                dve.wait_ge(s_yp, j + 1)
                if scattered is not None:
                    dve.wait_ge(s_ys[slot], scattered)
                V.tensor_copy(yy[:, slot, :], PS[:, 6 + r, 0:D]).then_inc(s_y, 1)

            def step(s, u):
                fixed = isinstance(s, int)
                if not fixed or 1 <= s <= BLOCKS:
                    hidden(s - 1, (u - 1) % 2, (u - 1) % NXS)
                if not fixed or 3 <= s:
                    j = s - 3
                    if fixed:
                        scattered = 16 * (j // NY) if j >= NY else None
                    else:
                        scattered = (s - u) * (16 // NY) + 16 * ((u - 3) // NY)
                    block_out(j, (u - 3) % 2, (u - 3) % NY, scattered)

            for s in range(NXS):
                step(s, s)
            with dve.Fori(NXS, BLOCKS, NXS) as i:
                for u in range(NXS):
                    step(i + u, u)
            for s in range(BLOCKS, BLOCKS + 3):
                step(s, s)
            for b in range(2, B):
                shared(b)
            cmb = PAY[:, :, :, :].rearrange("p t k r -> p (t k r)")
            for n in range(NT):
                o = (n % 4) * TOPK * D
                dve.wait_ge(s_cin[n % 4], 16 * (n // 4 + 1))
                c.add(TT(cmb[:, o:o + 3 * D], cmb[:, o:o + 3 * D], cmb[:, o + 3 * D:o + 6 * D], AD))
                c.wait()
                c.add(TT(cmb[:, o:o + D], cmb[:, o:o + D], cmb[:, o + D:o + 2 * D], AD))
                c.add(TT(cmb[:, o + 2 * D:o + 3 * D], cmb[:, o + 2 * D:o + 3 * D], resid[:, n, :], AD))
                c.wait()
                TT(resid[:, n, :], cmb[:, o:o + D], cmb[:, o + 2 * D:o + 3 * D], AD).then_inc(s_fin, 1)

        @block.tensor
        def _(pe):
            mm = nc.tensor.matmul

            def project(b):
                pe.wait_ge(s_xn, b + 1)
                at_least(pe, s_xnt, b)
                at_least(pe, s_xn2, b - 2)
                for t in range(TS):
                    for k in range(KD):
                        ins = nc.tensor.transpose(PS[:, k, t * P:(t + 1) * P], XN[:, t * D + k * P:t * D + (k + 1) * P], ident[:])
                ins.then_inc(s_xntp, 1)
                pe.wait_ge(s_xnt, b + 1)
                at_least(pe, s_xh, 2 * b)
                at_least(pe, s_dest, b - 2)
                at_least(pe, s_sc, b - 2)
                for m in range(KD):
                    for k in range(KD):
                        ins = mm(PS[:, 2 + m, :], w_in_s[:, k, m * P:(m + 1) * P], XNT[:, k * SEQ:(k + 1) * SEQ],
                                 start=(k == 0), stop=(k == KD - 1))
                ins.then_inc(s_xhp, 1)
                pe.wait_ge(s_xh, 2 * b + 2)
                at_least(pe, s_gates, 2 * b)
                for g in range(2):
                    for k in range(KD):
                        ins = mm(PS[:, 4 + g, :], bd[:, g, k, :], XH[b % 2][:, k * SEQ:(k + 1) * SEQ],
                                 start=(k == 0), stop=(k == KD - 1))
                ins.then_inc(s_gp, 1)

            def route(b):
                pe.wait_ge(s_pay, b + 1)
                pe.wait_ge(s_xnt, min(b + 3, B))
                at_least(pe, s_xn2, b)
                for t in range(TS):
                    for k in range(KD):
                        ins = nc.tensor.transpose(PS[:, k, t * P:(t + 1) * P], PAY[:, t, 0, k * P:(k + 1) * P], ident[:])
                ins.then_inc(s_xn2p, 1)
                pe.wait_ge(s_xn2, b + 1)
                pe.wait_ge(s_xh, 2 * min(b + 3, B))
                at_least(pe, s_sc, b)
                for t in range(TS):
                    for k in range(KD):
                        ins = mm(PS[:, 2, t * E:(t + 1) * E], XN2T[:, b, k, t * P:(t + 1) * P], gwt_s[:, k, :],
                                 start=(k == 0), stop=(k == KD - 1))
                ins.then_inc(s_lgp, 1)

            def out_project(b):
                pe.wait_ge(s_prod, b + 1)
                at_least(pe, s_x1, b)
                parts = ((T[1], w_out_s[:, 0, :]), (T[2], w_out_n[:]), (T[4], w_out_s[:, 1, :]), (T[5], w_out_s[:, 1, :]))
                for t in range(TS):
                    for n, (h, w) in enumerate(parts):
                        ins = mm(PS[:, 6 + t // 2, (t % 2) * D:(t % 2 + 1) * D], h[:, t * P:(t + 1) * P], w,
                                 start=(n == 0), stop=(n == len(parts) - 1))
                ins.then_inc(s_outp, 1)

            def positions(b):
                pe.wait_ge(s_memb, b + 1)
                at_least(pe, s_dest, b)
                for t in range(TS):
                    for v in range(t + 1):
                        mm(PS[:, 3, t * E:(t + 1) * E], (tri if v == t else ones)[:], memb[:, v, :], start=(v == 0), stop=(v == t))
                for v in range(TS):
                    ins = mm(PS[:, 3, TS * E:TS * E + E], ones[:], memb[:, v, :], start=(v == 0), stop=(v == TS - 1))
                ins.then_inc(s_posp, 1)

            pe.wait_ge(s_const, 9)
            pe.wait_ge(s_small, 80)
            pe.wait_ge(s_gatew, 256)
            pe.wait_ge(s_chan, 2)
            project(0)
            for b in range(B + 1):
                if b + 1 < B:
                    project(b + 1)
                if b >= 1:
                    route(b - 1)
                if b < B:
                    out_project(b)
                if b >= 1:
                    positions(b - 1)
            pe.wait_ge(s_tabf, 1)
            mm(PS[0:1, 0, 0:P], tabf[:, 2:3], ident[:], start=True, stop=True)
            mm(PS[0:1, 0, P:2 * P], tabf[:, 3:4], ident[:], start=True, stop=True).then_inc(s_tabp, 1)

            def shared(b):
                pe.wait_ge(s_dest, B)
                at_least(pe, s_shh, b)
                for h in range(KD):
                    for g in range(2):
                        for k in range(KD):
                            ins = mm(PS[:, 2 + 2 * g + h, :], sw13_s[:, k, g, h * P:(h + 1) * P], XN2T[:, b, k, :],
                                     start=(k == 0), stop=(k == KD - 1))
                ins.then_inc(s_shgp, 1)
                pe.wait_ge(s_shh, b + 1)
                at_least(pe, s_resid, b)
                for t in range(TS):
                    for h in range(KD):
                        ins = mm(PS[:, 6 + t // 2, (t % 2) * D:(t % 2 + 1) * D], SHG[:, h * SEQ + t * P:h * SEQ + (t + 1) * P],
                                 sw2_s[:, h, :], start=(h == 0), stop=(h == KD - 1))
                ins.then_inc(s_shyp, 1)

            pe.wait_ge(s_shw, 32)
            for b in range(2):
                shared(b)
            pe.wait_ge(s_resid, 2)
            pe.wait_ge(s_tab, 1)
            pe.wait_ge(s_wearly, 16)
            pe.wait_ge(s_wlate, 16)

            def expert_of(j):
                return pe.value_load(tabs[0:1, bass.ds(j + P, 1)], min_val=0, max_val=(E - 1) * EW)

            def rows_t(j, r, slot, loads):
                pe.wait_ge(s_xs[slot], loads)
                if not isinstance(j, int) or j >= 2:
                    pe.wait_ge(s_xt, j - 1)
                for k in range(KD):
                    ins = nc.tensor.transpose(PS[:, r, k * P:(k + 1) * P], xs[:, slot, k * P:(k + 1) * P], ident[:])
                ins.then_inc(s_xtp, 1)

            def gate_up(j, r):
                w = expert_of(j)
                pe.wait_ge(s_xt, j + 1)
                if not isinstance(j, int) or j >= 2:
                    pe.wait_ge(s_hh, j - 1)
                for k in range(KD):
                    ins = mm(PS[:, 2 + r, 0:2 * P], xT[:, r, k * P:(k + 1) * P], W[:, bass.ds(w + k * 2 * P, 2 * P)],
                             start=(k == 0), stop=(k == KD - 1))
                ins.then_inc(s_gup, 1)

            def hidden_t(j, r):
                pe.wait_ge(s_hh, j + 1)
                if not isinstance(j, int) or j >= 2:
                    pe.wait_ge(s_ht, j - 1)
                nc.tensor.transpose(PS[:, 4 + r, 0:P], hh[:, r, :], ident[:]).then_inc(s_hp, 1)

            def down(j, r):
                w = expert_of(j)
                pe.wait_ge(s_ht, j + 1)
                if not isinstance(j, int) or j >= 2:
                    pe.wait_ge(s_y, j - 1)
                mm(PS[:, 6 + r, 0:D], hT[:, r, :], W[:, bass.ds(w + KD * 2 * P, D)], start=True, stop=True).then_inc(s_yp, 1)

            def step(s, u):
                fixed = isinstance(s, int)
                if not fixed or 1 <= s <= BLOCKS:
                    gate_up(s - 1, (u - 1) % 2)
                if not fixed or 3 <= s:
                    down(s - 3, (u - 3) % 2)
                if not fixed or 2 <= s <= BLOCKS + 1:
                    hidden_t(s - 2, u % 2)
                if not fixed or s < BLOCKS:
                    loads = 16 * (s // NXS + 1) if fixed else (s - u) * (16 // NXS) + 16
                    rows_t(s, u % 2, u % NXS, loads)

            for s in range(NXS):
                step(s, s)
            with pe.Fori(NXS, BLOCKS, NXS) as i:
                for u in range(NXS):
                    step(i + u, u)
            for s in range(BLOCKS, BLOCKS + 3):
                step(s, s)
            pe.wait_ge(s_y, BLOCKS)
            for b in range(2, B):
                shared(b)


_LAUNCH = ["x", "chan", "w_in", "w_gx", "w_ga", "w_out", "b_out", "gate_wt", "experts", "sw13", "sw2"]


def kernel(**inputs):
    import numpy as _np
    import concourse.bacc as _bacc
    from concourse import mybir as _mybir
    from concourse.bass_utils import run_bass_kernel_spmd as _run

    a = {k: _np.asarray(v) for k, v in inputs.items()}
    P = 128
    chan = _np.stack([a["L0_attn_b_in"][:P], a["L0_attn_b_in"][P:], a["L0_attn_b_gx"].reshape(P), a["L0_attn_b_ga"].reshape(P),
                      a["L0_attn_a_real"], a["L0_attn_a_imag"]], axis=1)
    E, F, D = a["L0_ffn_w11"].shape
    K = D // P
    w13 = _np.stack([a["L0_ffn_w11"], a["L0_ffn_w33"]])
    w13 = w13.reshape(2, E, F, K, P).transpose(4, 1, 3, 0, 2).reshape(P, E, K * 2 * F)
    w2 = a["L0_ffn_w22"].transpose(2, 0, 1)
    sw13 = _np.stack([a["L0_ffn_sw1"], a["L0_ffn_sw3"]])
    sw13 = sw13.reshape(2, sw13.shape[1], K, P).transpose(3, 2, 0, 1)
    sw2 = a["L0_ffn_sw2"].T.reshape(K, P, D).transpose(1, 0, 2)
    laid = dict(x=a["L0_attn_x"], chan=chan, w_in=a["L0_attn_W_in"], w_gx=a["L0_attn_W_gx"], w_ga=a["L0_attn_W_ga"],
                w_out=a["L0_attn_W_out"], b_out=a["L0_attn_b_out"],
                gate_wt=a["L0_ffn_gate_w"].T.reshape(K, P, E).transpose(1, 0, 2),
                experts=_np.concatenate([w13, w2], axis=2), sw13=sw13, sw2=sw2)
    nc = _bacc.Bacc("TRN2", target_bir_lowering=False, num_devices=1)
    arrays, args = {}, []
    for name in _LAUNCH:
        v = _np.ascontiguousarray(laid[name])
        arrays[f"in_{name}"] = v
        args.append(nc.dram_tensor(f"in_{name}", v.shape, _mybir.dt.from_np(v.dtype), kind="ExternalInput").ap())
    shape = a["L0_attn_x"].shape
    args.append(nc.dram_tensor("out_0", shape, _mybir.dt.float32, kind="ExternalOutput").ap())
    preln_recurrence_moe(nc, *args)
    r = _run(nc, [arrays], core_ids=[0])
    return r.results[0]["out_0"]
```

```python
import concourse.bass as bass
from concourse import mybir
from concourse.alu_op_type import AluOpType as ALU
from contextlib import ExitStack
import math


def preln_recurrence_moe(nc, x, chan, w_in, gate_bd, w_out, b_out, gate_wt, experts, sw13, sw2, out):
    f32 = mybir.dt.float32
    bf16 = mybir.dt.bfloat16
    i32 = mybir.dt.int32
    u32 = mybir.dt.uint32
    ACT = mybir.ActivationFunctionType
    X = mybir.AxisListType.X

    B, SEQ, D = x.shape
    N = B * SEQ
    P = 128
    KD = D // P
    TS = SEQ // P
    NT = N // P
    E, GRP, TOPG, TOPK = 32, 8, 4, 6
    PER = E // GRP
    ROUTE_SCALE = 2.5
    EPS = 1e-5
    CAP = N + P
    PADROW = E * CAP
    ROW = D + 2
    BLOCKS = N * TOPK // P + E
    EW = KD * 2 * P + D
    SHARED_BEFORE = B - 1
    NXS = 8
    NY = 4
    SKIP = 1 << 20
    MAGIC = 1.5 * 2.0 ** 23
    TWO_PI = 6.283185
    LN2H = 0.5 * math.log(2.0)

    xt_d = x.rearrange("b (t p) d -> b p t d", p=P)
    out_d = out.rearrange("b (t p) d -> (b t) p d", p=P)
    bucket = nc.dram_tensor("bucket_rows", (E * CAP + P, ROW), f32)
    choice = nc.dram_tensor("choice_rows", (N * TOPK, D), f32)
    bucket_ap = bucket.ap()
    choice_ap = choice.ap()
    choice_t = choice_ap.rearrange("(n p k) d -> n p (k d)", p=P, k=TOPK)

    ctx = ExitStack()
    with ctx:
        def sb(name, shape, dt=f32):
            return ctx.enter_context(nc.sbuf_tensor(name, shape, dt))

        def sem(name):
            return ctx.enter_context(nc.semaphore(name))

        W = sb("expert_weights", [P, E * EW])
        UNITS = 40
        EARLY = (E * EW - UNITS * SEQ) // EW
        base = E * EW - UNITS * SEQ

        def unit(u, k=1):
            return W[:, base + u * SEQ: base + (u + k) * SEQ]

        XH = [unit(0, 2), unit(2, 2)]
        SN = [unit(4, 2), unit(6, 2)]
        CS = [unit(8, 2), unit(10, 2)]
        GX = [unit(12), unit(13)]
        RHO = [unit(14), unit(15)]
        T = [unit(16 + i) for i in range(8)]
        XNT = unit(24, 2)
        FR = unit(26, 2)
        XN = unit(28, 2)
        AB = sb("turn_abs", [P, 2 * SEQ])
        GU = unit(30, 2)
        RHO2 = unit(32)
        E2 = unit(33)
        Q = unit(34)
        W1 = unit(35)
        ZR = unit(36)
        M2 = unit(37)
        SR = unit(38)
        RR = unit(39)

        resid = sb("resid", [P, NT, D])
        XN2T = sb("xn2_t", [P, B, KD, SEQ])
        PAYS = sb("payload", [P, 2 * TS, TOPK, ROW])
        PAY = [PAYS[:, 0:TS, :, :], PAYS[:, TS:2 * TS, :, :]]
        PADT = sb("pad_rows", [P, ROW])
        w_in_s = sb("w_in_s", [P, KD, D])
        w_out_s = sb("w_out_s", [P, KD, D])
        w_out_n = sb("w_out_n", [P, D])
        bd = sb("gate_blockdiag", [P, 2, KD, P])
        sw13_s = sb("sw13_s", [P, KD, 2, D])
        sw2_s = sb("sw2_s", [P, KD, D])
        gwt_s = sb("gwt_s", [P, KD, E])
        bout_s = sb("bout_s", [P, D])
        chan_s = sb("chan_s", [P, 6])
        ident = sb("ident", [P, P])
        tri = sb("tri", [P, P], bf16)
        ones = sb("ones", [P, P], bf16)
        iota_g = sb("iota_g", [P, GRP])
        iota_e = sb("iota_e", [P, E])
        iota_p = sb("iota_p", [P, 1])
        thr = sb("thr", [P, NT])
        cb0 = sb("bucket_base", [P, E])
        cb = sb("bucket_next", [P, E])
        cst = sb("consts", [P, 4])
        ch = sb("chan_derived", [P, 10])
        st1 = sb("st1", [P, B, TS, 6])
        st2 = sb("st2", [P, B, TS, 6])
        mv1 = sb("mv1", [P, B, TS, 2])
        rs1 = sb("rs1", [P, B, 2, TS])
        mv2 = sb("mv2", [P, B, TS, 2])
        rs2 = sb("rs2", [P, B, 2, TS])
        sc = sb("scores", [P, TS, E])
        sc2 = sb("scores_tmp", [P, TS, E])
        gm = sb("group_max", [P, TS, GRP])
        gv = sb("gv", [P, TS, 8])
        gi = sb("gi", [P, TS, 8], u32)
        gif = sb("gif", [P, TS, TOPG])
        geq = sb("geq", [P, TS, GRP, TOPG])
        gmask = sb("gmask", [P, TS, GRP])
        gmm = sb("gmm", [P, TS, GRP])
        msk = sb("masked", [P, TS, E])
        ev = sb("ev", [P, TS, 8])
        ei = sb("ei", [P, TS, 8], u32)
        eif = sb("eif", [P, TS, TOPK])
        wsum = sb("wsum", [P, 2, TS])
        oh = sb("one_hot", [P, TS * TOPK, E])
        memb = sb("member", [P, TS, E], bf16)
        dpos = sb("dpos", [P, TS, E])
        dest = sb("dest", [P, 2, TS * TOPK], i32)
        destf = sb("destf", [P, TS * TOPK])
        cnt = sb("cnt", [P, 6, E])
        zero_e = sb("zero_e", [P, E])
        cmpb = oh[:].rearrange("p q e -> p (q e)")[:, 0:E * NT].rearrange("p (e n) -> p e n", n=NT)
        tabf = sb("tabf", [P, 4])
        tabs = sb("tabs", [1, 2 * P + E], i32)
        at = [TS * TOPK * ROW]
        flat = PAYS[:, :, :, :].rearrange("p t k r -> p (t k r)")

        def over_payload(n, w):
            at[0] += n * w
            return flat[:, at[0] - n * w:at[0]].rearrange("p (n w) -> p n w", w=w)

        xs = over_payload(NXS, ROW)
        xT = over_payload(2, D)
        sg = over_payload(2, P)
        hh = over_payload(2, P)
        hT = over_payload(2, P)
        yy = over_payload(NY, D)
        xs_idx = xs.bitcast(i32)
        NC = 2 * TS * TOPK * ROW // (TOPK * D)
        SHG = AB

        PS = ctx.enter_context(nc.psum_tensor("PS", [P, 8, 512], f32))

        s_x = [sem(f"x_loaded{b}") for b in range(B)]
        s_win = sem("w_in_loaded")
        s_chw = sem("channel_vectors_loaded")
        s_gatew = sem("gate_weights_loaded")
        s_small = sem("small_weights_loaded")
        s_shw = sem("shared_weights_loaded")
        s_wearly = sem("early_experts_loaded")
        s_wlate = sem("late_experts_loaded")
        s_const = sem("constants_built")
        s_bout = sem("output_bias_added")
        s_dve = sem("dve_chain")
        s_act = sem("act_chain")
        s_pool = sem("pool_chain")
        s_spin = sem("softplus_input")
        s_spout = sem("softplus_log")
        s_chan = sem("channel_constants")
        s_stats1 = sem("ln1_stats")
        s_rstd1 = sem("ln1_rstd")
        s_xn = sem("ln1_rows")
        s_xntp = sem("ln1_transposed_psum")
        s_xnt = sem("ln1_transposed")
        s_xhp = sem("projected_psum")
        s_xh = sem("projected")
        s_gp = sem("gates_psum")
        s_gates = sem("gates")
        s_rho = sem("decay_ready")
        s_turn = sem("turns_reduced")
        s_trig = sem("sines_ready")
        s_m2 = sem("z_squared_abs")
        s_zabs = sem("z_abs_ready")
        s_zt = sem("z_abs_plus_re")
        s_zroot = sem("z_root_ready")
        s_xused = sem("projection_used")
        s_prod = sem("rotated_products")
        s_outp = sem("attention_out_psum")
        s_x1 = sem("first_residual")
        s_stats2 = sem("ln2_stats")
        s_rstd2 = sem("ln2_rstd")
        s_pay = sem("ln2_rows")
        s_xn2p = sem("ln2_transposed_psum")
        s_xn2 = sem("ln2_transposed")
        s_lgp = sem("router_logits_psum")
        s_sc = sem("router_scores")
        s_memb = sem("membership")
        s_posp = sem("positions_psum")
        s_dest = sem("bucket_rows_known")
        s_rep = sem("ln2_rows_repeated")
        s_rowid = sem("output_row_ids")
        s_scat = [sem(f"rows_scattered{b}") for b in range(B)]
        s_tabf = sem("block_table_columns")
        s_tabp = sem("block_table_psum")
        s_tab = sem("block_table")
        s_padt = sem("padding_tile")
        s_pad = sem("padding_written")
        s_shgp = sem("shared_gate_up_psum")
        s_shs = sem("shared_silu")
        s_shh = sem("shared_hidden")
        s_shyp = sem("shared_out_psum")
        s_resid = sem("second_residual")
        s_xs = [sem(f"block_rows{i}") for i in range(NXS)]
        s_xtp = sem("block_transposed_psum")
        s_xt = sem("block_transposed")
        s_gup = sem("block_gate_up_psum")
        s_sg = sem("block_silu")
        s_hh = sem("block_hidden")
        s_hp = sem("hidden_transposed_psum")
        s_ht = sem("hidden_transposed")
        s_yp = sem("block_out_psum")
        s_y = sem("block_out")
        s_ys = [sem(f"block_scattered{i}") for i in range(NY)]
        s_cin = [sem(f"choices_loaded{i}") for i in range(NC)]
        s_fin = sem("token_summed")
        s_out = [sem(f"token_stored{i}") for i in range(4)]

        block = ctx.enter_context(nc.Block())

        class Chain:

            def __init__(self, eng, s):
                self.eng, self.s, self.n = eng, s, 0

            def add(self, ins):
                ins.then_inc(self.s, 1)
                self.n += 1

            def wait(self):
                self.eng.wait_ge(self.s, self.n)

        def at_least(eng, s, n):
            if n > 0:
                eng.wait_ge(s, n)

        def tiles(b):
            return slice(b * TS, (b + 1) * TS)

        @block.sync
        def _(sp):
            for b in range(B):
                sp.dma_start(resid[:, tiles(b), :], xt_d[b]).then_inc(s_x[b], 16)
                if b == 0:
                    sp.dma_start(w_in_s[:], w_in.rearrange("(k p) n -> p k n", p=P)).then_inc(s_win, 16)
            sp.dma_start(W[:, 0:EARLY * EW].rearrange("p (e w) -> p e w", w=EW), experts[:, 0:EARLY, :]).then_inc(s_wearly, 16)
            sp.dma_start(sw13_s[:], sw13).then_inc(s_shw, 16)
            sp.dma_start(sw2_s[:], sw2).then_inc(s_shw, 16)
            sp.wait_ge(s_padt, 3)
            sp.dma_start(bucket_ap[PADROW:PADROW + P, :], PADT[:]).then_inc(s_pad, 16)
            sp.wait_ge(s_outp, B)
            sp.wait_ge(s_prod, B)
            sp.wait_ge(s_zroot, B)
            sp.dma_start(W[:, EARLY * EW:].rearrange("p (e w) -> p e w", w=EW), experts[:, EARLY:, :]).then_inc(s_wlate, 16)
            sp.wait_ge(s_tab, 1)
            for e in range(E):
                row = sp.value_load(tabs[0:1, 2 * P + e:2 * P + e + 1], min_val=0, max_val=E * CAP)
                sp.dma_start(bucket_ap[bass.ds(row, P), :], PADT[:]).then_inc(s_pad, 16)
            sp.wait_ge(s_pad, 16 * (E + 1))
            for b in range(B):
                sp.wait_ge(s_scat[b], 16 * TS * TOPK)

            def load_block(j, slot, tail_rounds):
                if tail_rounds is not None:
                    sp.wait_ge(s_ys[slot % NY], tail_rounds)
                row = sp.value_load(tabs[0:1, bass.ds(j, 1)], min_val=0, max_val=E * CAP)
                sp.dma_start(xs[:, slot, :], bucket_ap[bass.ds(row, P), :]).then_inc(s_xs[slot], 16)

            for j in range(NXS):
                load_block(j, j, None)
            with sp.Fori(NXS, BLOCKS, NXS) as i:
                for u in range(NXS):
                    load_block(i + u, u, (i - NXS) * (16 // NY) + 16 * (u // NY + 1))
            for q in range(NY):
                sp.wait_ge(s_ys[q], 16 * (BLOCKS // NY))
            for n in range(NT):
                if n >= NC:
                    sp.wait_ge(s_fin, n - NC + 1)
                sp.dma_start(flat[:, (n % NC) * TOPK * D:(n % NC + 1) * TOPK * D], choice_t[n]).then_inc(s_cin[n % NC], 16)

        @block.gpsimd
        def _(pool):
            pch = Chain(pool, s_pool)
            pch.add(nc.gpsimd.memset(ident[:], 0.0))
            pch.add(nc.gpsimd.memset(tri[:], 1.0))
            pch.wait()
            nc.gpsimd.affine_select(out=ident[:], in_=ident[:], compare_op=ALU.not_equal, fill=1.0, base=0,
                                    pattern=[[-1, P]], channel_multiplier=1).then_inc(s_const, 1)
            nc.gpsimd.affine_select(out=tri[:], in_=tri[:], compare_op=ALU.is_gt, fill=0.0, base=0,
                                    pattern=[[1, P]], channel_multiplier=-1).then_inc(s_const, 1)
            nc.gpsimd.memset(ones[:], 1.0).then_inc(s_const, 1)
            nc.gpsimd.iota(iota_g[:], pattern=[[1, GRP]], base=0, channel_multiplier=0,
                           allow_small_or_imprecise_dtypes=True).then_inc(s_const, 1)
            nc.gpsimd.iota(iota_e[:], pattern=[[1, E]], base=0, channel_multiplier=0,
                           allow_small_or_imprecise_dtypes=True).then_inc(s_const, 1)
            nc.gpsimd.iota(iota_p[:], pattern=[[0, 1]], base=0, channel_multiplier=1,
                           allow_small_or_imprecise_dtypes=True).then_inc(s_const, 1)
            nc.gpsimd.iota(thr[:], pattern=[[P, NT]], base=0, channel_multiplier=0,
                           allow_small_or_imprecise_dtypes=True).then_inc(s_const, 1)
            nc.gpsimd.iota(cb0[:], pattern=[[CAP, E]], base=0, channel_multiplier=0,
                           allow_small_or_imprecise_dtypes=True).then_inc(s_const, 1)
            nc.gpsimd.memset(zero_e[:], 0.0).then_inc(s_const, 1)
            nc.gpsimd.memset(PADT[:, 0:D], 0.0).then_inc(s_padt, 1)
            nc.gpsimd.memset(PADT[:, D + 1:D + 2], 0.0).then_inc(s_padt, 1)
            nc.gpsimd.iota(PADT[:, D:D + 1].bitcast(i32), pattern=[[0, 1]], base=SKIP,
                           channel_multiplier=0).then_inc(s_padt, 1)
            pool.wait_ge(s_small, 48)
            for b in range(B):
                pool.wait_ge(s_xn, b + 1)
                nc.gpsimd.tensor_tensor(resid[:, tiles(b), :], resid[:, tiles(b), :],
                                        bout_s[:].unsqueeze(1).to_broadcast([P, TS, D]), ALU.add).then_inc(s_bout, 1)

            def row_ids(b):
                if b >= 2:
                    pool.wait_ge(s_scat[b - 2], 16 * TS * TOPK)
                nc.gpsimd.iota(PAY[b % 2].bitcast(i32)[:, :, :, D], pattern=[[P * TOPK, TS], [1, TOPK]], base=b * SEQ * TOPK,
                               channel_multiplier=TOPK).then_inc(s_rowid, 1)

            def scatter_rows(b):
                pool.wait_ge(s_rowid, b + 1)
                pool.wait_ge(s_rep, b + 1)
                pool.wait_ge(s_dest, b + 1)
                for t in range(TS):
                    for k in range(TOPK):
                        q = t * TOPK + k
                        nc.gpsimd.indirect_dma_start(
                            out=bucket_ap[:, :], out_offset=bass.IndirectOffsetOnAxis(ap=dest[:, b % 2, q:q + 1], axis=0),
                            in_=PAY[b % 2][:, t, k, :], in_offset=None).then_inc(s_scat[b], 16)

            row_ids(0)
            row_ids(1)
            scatter_rows(0)
            for b in range(1, B):
                scatter_rows(b)
                if b + 1 < B:
                    row_ids(b + 1)

            zero, last, last_row = (pool.alloc_register(n) for n in ("row_zero", "row_last", "row_bound"))
            pool.reg_mov(zero, 0)
            pool.reg_mov(last, N * TOPK - 1)

            def scatter(j, slot, ready):
                pool.wait_ge(s_y, ready)
                pool.reg_add(last_row, zero, last)
                nc.gpsimd.indirect_dma_start(
                    out=choice_ap[:, :], out_offset=bass.IndirectOffsetOnAxis(ap=xs_idx[:, slot, D:D + 1], axis=0),
                    in_=yy[:, slot % NY, :], in_offset=None,
                    bounds_check=last_row, oob_is_err=False).then_inc(s_ys[slot % NY], 16)

            with pool.Fori(0, BLOCKS, NXS) as i:
                for u in range(NXS):
                    scatter(i + u, u, i + u + 1)

        @block.scalar
        def _(act):
            ach = Chain(act, s_act)
            A = nc.scalar.activation

            tables = nc.scalar.preload_act_table_set
            EXP_LN, SILU = "natural_log_exp_and_others", "silu_and_others"

            def rstd(mv, rs, s_in, s_out, b):
                act.wait_ge(s_in, b + 1)
                ach.add(A(rs[:, b, 0, :], mv[:, b, :, 1], ACT.Ln, bias=cst[:, 2:3]))
                ach.wait()
                A(rs[:, b, 1, :], rs[:, b, 0, :], ACT.Exp, scale=-0.5).then_inc(s_out, 1)

            def rstd1(b):
                rstd(mv1, rs1, s_stats1, s_rstd1, b)

            def rstd2(b):
                rstd(mv2, rs2, s_stats2, s_rstd2, b)

            def ln1_transposed(b):
                act.wait_ge(s_xntp, b + 1)
                at_least(act, s_xhp, b)
                A(XNT, PS[:, 0:2, :], ACT.Copy).then_inc(s_xnt, 1)

            def projected(b):
                p = b % 2
                act.wait_ge(s_xhp, b + 1)
                at_least(act, s_xused, b - 1)
                for k in range(KD):
                    A(XH[p][:, k * SEQ:(k + 1) * SEQ], PS[:, 2 + k, :], ACT.Identity,
                      bias=chan_s[:, k:k + 1]).then_inc(s_xh, 1)

            def gates(b):
                p = b % 2
                act.wait_ge(s_gp, b + 1)
                A(GX[p], PS[:, 4, :], ACT.Sigmoid, bias=chan_s[:, 2:3]).then_inc(s_gates, 1)
                at_least(act, s_turn, b)
                A(GU[:, 0:SEQ], PS[:, 5, :], ACT.Sigmoid, bias=chan_s[:, 3:4]).then_inc(s_gates, 1)

            def decay(b):
                p = b % 2
                tables(EXP_LN)
                act.wait_ge(s_gates, 2 * b + 2)
                at_least(act, s_prod, b - 1)
                at_least(act, s_m2, b)
                if b == 0:
                    act.wait_ge(s_chan, 1)
                A(RHO[p], GU[:, 0:SEQ], ACT.Exp, scale=ch[:, 1:2]).then_inc(s_rho, 1)
                ach.add(A(RHO2, GU[:, 0:SEQ], ACT.Exp, scale=ch[:, 2:3]))
                ach.wait()
                A(E2, RHO2, ACT.Square, scale=-1.0, bias=1.0).then_inc(s_rho, 1)

            def sines(b):
                p = b % 2
                act.wait_ge(s_turn, b + 1)
                A(SN[p], FR, ACT.Sin, scale=TWO_PI)
                A(CS[p], AB[:], ACT.Sin, scale=-TWO_PI, bias=cst[:, 0:1]).then_inc(s_trig, 1)

            def zabs(b):
                act.wait_ge(s_m2, b + 1)
                ach.add(A(M2, M2, ACT.Ln, bias=cst[:, 1:2]))
                ach.wait()
                A(M2, M2, ACT.Exp, scale=0.5).then_inc(s_zabs, 1)

            def zroots(b):
                act.wait_ge(s_zt, b + 1)
                ach.add(A(M2, M2, ACT.Ln))
                ach.wait()
                A(SR, M2, ACT.Exp, scale=0.5, bias=cst[:, 3:4])
                A(RR, M2, ACT.Exp, scale=-0.5, bias=cst[:, 3:4]).then_inc(s_zroot, 1)

            def ln2_transposed(b):
                act.wait_ge(s_xn2p, b + 1)
                A(XN2T[:, b, :, :], PS[:, 0:2, :], ACT.Copy).then_inc(s_xn2, 1)

            def repeat_rows(b):
                act.wait_ge(s_pay, b + 1)
                for t in range(TS):
                    ins = A(PAY[b % 2][:, t, 1:TOPK, 0:D],
                            PAY[b % 2][:, t, 0, 0:D].unsqueeze(1).to_broadcast([P, TOPK - 1, D]), ACT.Copy)
                ins.then_inc(s_rep, 1)

            def scores(b):
                act.wait_ge(s_lgp, b + 1)
                at_least(act, s_memb, b)
                ach.add(A(sc2[:], PS[:, 2, 0:TS * E].rearrange("p (t e) -> p t e", e=E), ACT.Exp, scale=-1.0))
                ach.wait()
                ach.add(A(sc2[:], sc2[:], ACT.Ln, bias=1.0))
                ach.wait()
                A(sc[:, :, :], sc2[:], ACT.Exp, scale=-1.0).then_inc(s_sc, 1)

            act.dma_start(chan_s[:], chan).then_inc(s_chw, 16)
            act.dma_start(bd[:], gate_bd).then_inc(s_gatew, 16)
            act.dma_start(bout_s[:], b_out.partition_broadcast(P)).then_inc(s_small, 16)
            act.dma_start(w_out_s[:], w_out.rearrange("(k p) n -> p k n", p=P)).then_inc(s_small, 16)
            act.dma_start(gwt_s[:], gate_wt).then_inc(s_small, 16)
            tables(EXP_LN)
            act.wait_ge(s_spin, 1)
            ach.add(A(ch[:, 4:5], ch[:, 3:4], ACT.Exp, scale=-1.0))
            ach.wait()
            A(ch[:, 5:6], ch[:, 4:5], ACT.Ln, bias=1.0).then_inc(s_spout, 1)
            for stage, b in (
                    (rstd1, 0), (rstd1, 1), (ln1_transposed, 0), (rstd1, 2), (rstd1, 3), (projected, 0), (ln1_transposed, 1),
                    (gates, 0), (decay, 0), (projected, 1), (sines, 0), (tables, EXP_LN), (zabs, 0), (zroots, 0),
                    (gates, 1), (decay, 1), (sines, 1), (ln1_transposed, 2), (projected, 2), (gates, 2), (decay, 2),
                    (zabs, 1), (zroots, 1), (rstd2, 0), (sines, 2), (tables, EXP_LN), (ln2_transposed, 0), (scores, 0),
                    (repeat_rows, 0), (zabs, 2), (zroots, 2), (ln1_transposed, 3), (rstd2, 1), (projected, 3), (ln2_transposed, 1),
                    (scores, 1), (gates, 3), (decay, 3), (sines, 3), (repeat_rows, 1), (tables, EXP_LN), (zabs, 3), (zroots, 3),
                    (rstd2, 2), (ln2_transposed, 2), (scores, 2), (repeat_rows, 2),
                    (rstd2, 3), (ln2_transposed, 3), (scores, 3), (repeat_rows, 3)):
                stage(b)

            def shared(b):
                act.wait_ge(s_shgp, b + 1)
                at_least(act, s_shyp, b)
                A(SHG[:].rearrange("p (h n) -> p h n", h=KD), PS[:, 2:4, :], ACT.Silu).then_inc(s_shs, 1)

            def silu(j, r):
                act.wait_ge(s_gup, j + 1)
                if not isinstance(j, int) or j >= 2:
                    act.wait_ge(s_hh, j - 1)
                A(sg[:, r, :], PS[:, 2 + r, 0:P], ACT.Silu).then_inc(s_sg, 1)

            def hidden_t(j, r):
                act.wait_ge(s_hp, j + 1)
                if not isinstance(j, int) or j >= 2:
                    act.wait_ge(s_yp, j - 1)
                A(hT[:, r, :], PS[:, 4 + r, 0:P], ACT.Copy).then_inc(s_ht, 1)

            def rows_t(j, r):
                act.wait_ge(s_xtp, j + 1)
                if not isinstance(j, int) or j >= 2:
                    act.wait_ge(s_gup, j - 1)
                A(xT[:, r, :], PS[:, r, 0:D], ACT.Copy).then_inc(s_xt, 1)

            tables(SILU)
            for b in range(SHARED_BEFORE):
                shared(b)

            def step(s, u):
                if not isinstance(s, int) or 2 <= s <= BLOCKS + 1:
                    silu(s - 2, u % 2)
                if not isinstance(s, int) or 3 <= s <= BLOCKS + 2:
                    hidden_t(s - 3, (u - 3) % 2)
                if not isinstance(s, int) or s < BLOCKS:
                    rows_t(s, u % 2)

            for s in range(NXS):
                step(s, s)
            with act.Fori(NXS, BLOCKS, NXS) as i:
                for u in range(NXS):
                    step(i + u, u)
            for s in range(BLOCKS, BLOCKS + 4):
                step(s, s)
            for b in range(SHARED_BEFORE, B):
                shared(b)
            for n in range(NT):
                act.wait_ge(s_fin, n + 1)
                act.dma_start(out_d[n], resid[:, n, :]).then_inc(s_out[n % 4], 16)
            for q in range(4):
                act.wait_ge(s_out[q], 16 * (NT // 4))

        @block.vector
        def _(dve):
            c = Chain(dve, s_dve)
            V = nc.vector
            TT, TSC, STT = V.tensor_tensor, V.tensor_scalar, V.scalar_tensor_tensor
            M, AD, SU = ALU.mult, ALU.add, ALU.subtract

            def stats(src, b, st, mv, s_out):
                for t in range(TS):
                    c.add(V.bn_stats(st[:, b, t, :], src[:, b * TS + t, :]))
                c.wait()
                for t in range(TS):
                    ins = V.bn_aggr(mv[:, b, t, :], st[:, b, t, :])
                ins.then_inc(s_out, 1)

            def ln1_stats(b):
                dve.wait_ge(s_x[b], 16)
                stats(resid, b, st1, mv1, s_stats1)

            def ln1_rows(b):
                dve.wait_ge(s_rstd1, b + 1)
                at_least(dve, s_xntp, b)
                for t in range(TS):
                    ins = TSC(XN[:, t * D:(t + 1) * D], resid[:, b * TS + t, :], mv1[:, b, t, 0:1], rs1[:, b, 1, t:t + 1], SU, M)
                ins.then_inc(s_xn, 1)

            def turns(b):
                dve.wait_ge(s_gates, 2 * b + 2)
                at_least(dve, s_trig, b)
                c.add(V.tensor_tensor_scan(GU[:, SEQ:], GU[:, 0:SEQ], GU[:, 0:SEQ], 0.0, AD, ALU.bypass))
                c.wait()
                c.add(TSC(AB[:], GU, ch[:, 0:1], MAGIC, M, AD))
                c.wait()
                c.add(TSC(AB[:], AB[:], MAGIC, None, SU))
                c.wait()
                c.add(STT(FR, GU, ch[:, 0:1], AB[:], M, SU))
                c.wait()
                TSC(AB[:].bitcast(i32), FR.bitcast(i32), 0x7FFFFFFF, None, ALU.bitwise_and).then_inc(s_turn, 1)

            def z_parts(b):
                p = b % 2
                s, co = SN[p][:, 0:SEQ], CS[p][:, 0:SEQ]
                dve.wait_ge(s_trig, b + 1)
                dve.wait_ge(s_rho, 2 * b + 2)
                c.add(STT(Q, s, 2.0, RHO2, M, M))
                c.wait()
                c.add(TT(W1, Q, s, M))
                c.add(TT(Q, Q, co, M))
                dve.wait_ge(s_dve, c.n - 1)
                c.add(STT(ZR, W1, 1.0, RHO2, AD, SU))
                STT(M2, W1, 2.0, E2, M, AD).then_inc(s_m2, 1)

            def z_sum(b):
                dve.wait_ge(s_zabs, b + 1)
                c.wait()
                c.add(TT(M2, M2, ZR, AD))
                c.wait()
                TSC(M2, M2, 1e-30, None, ALU.max).then_inc(s_zt, 1)

            def gate_input(b):
                p = b % 2
                dve.wait_ge(s_zroot, b + 1)
                dve.wait_ge(s_xh, 2 * b + 2)
                at_least(dve, s_outp, b)
                c.add(TT(Q, Q, RR, M))
                c.add(TT(T[0], XH[p][:, 0:SEQ], GX[p], M))
                ins = TT(T[1], XH[p][:, SEQ:], GX[p], M)
                ins.then_inc(s_xused, 1)
                c.wait()
                c.add(TT(T[2], T[0], SR, M))
                c.add(TT(T[5], T[0], Q, M))
                dve.wait_ge(s_xused, b + 1)
                c.add(TT(T[3], T[1], Q, M))
                c.add(TT(T[4], T[1], SR, M))
                dve.wait_ge(s_dve, c.n - 1)
                c.add(TT(T[2], T[2], T[3], AD))
                dve.wait_ge(s_dve, c.n - 1)
                c.add(TT(T[4], T[4], T[5], SU))

            def rotate_back(b):
                p = b % 2
                s, co = SN[p][:, SEQ:], CS[p][:, SEQ:]
                c.wait()
                c.add(TT(T[0], T[2], co, M))
                c.add(TT(T[1], T[4], s, M))
                c.add(TT(T[3], T[4], co, M))
                c.add(TT(T[5], T[2], s, M))
                dve.wait_ge(s_dve, c.n - 2)
                c.add(TT(T[0], T[0], T[1], AD))
                dve.wait_ge(s_dve, c.n - 1)
                c.add(TT(T[3], T[3], T[5], SU))

            def scan_rotate(b):
                p = b % 2
                s, co = SN[p][:, SEQ:], CS[p][:, SEQ:]
                c.wait()
                c.add(V.tensor_tensor_scan(T[6], RHO[p], T[0], 0.0, M, AD))
                c.add(V.tensor_tensor_scan(T[7], RHO[p], T[3], 0.0, M, AD))
                dve.wait_ge(s_dve, c.n - 1)
                TT(T[1], T[6], co, M)
                TT(T[4], T[6], s, M)
                c.wait()
                TT(T[2], T[7], s, M)
                TT(T[5], T[7], co, M).then_inc(s_prod, 1)

            def residual1(b):
                dve.wait_ge(s_outp, b + 1)
                dve.wait_ge(s_bout, b + 1)
                TT(resid[:, tiles(b), :], resid[:, tiles(b), :],
                   PS[:, 6:8, :].rearrange("p a (c d) -> p (a c) d", d=D), AD).then_inc(s_x1, 1)
                dve.wait_ge(s_x1, b + 1)
                stats(resid, b, st2, mv2, s_stats2)

            def ln2_rows(b):
                dve.wait_ge(s_rstd2, b + 1)
                if b >= 2:
                    dve.wait_ge(s_scat[b - 2], 16 * TS * TOPK)
                for t in range(TS):
                    ins = TSC(PAY[b % 2][:, t, 0, 0:D], resid[:, b * TS + t, :],
                              mv2[:, b, t, 0:1], rs2[:, b, 1, t:t + 1], SU, M)
                ins.then_inc(s_pay, 1)

            def choose(b):
                dve.wait_ge(s_sc, b + 1)
                c.add(V.tensor_reduce(gm[:], sc[:, :, :].rearrange("p t (g m) -> p t g m", m=PER), X, ALU.max))
                c.wait()
                for t in range(TS):
                    c.add(V.max(gv[:, t, :], gm[:, t, :]))
                c.wait()
                for t in range(TS):
                    c.add(V.max_index(gi[:, t, :], gv[:, t, :], gm[:, t, :]))
                c.wait()
                c.add(V.tensor_copy(gif[:], gi[:, :, 0:TOPG]))
                c.wait()
                for t in range(TS):
                    c.add(TT(geq[:, t, :, :], iota_g[:].unsqueeze(2).to_broadcast([P, GRP, TOPG]),
                             gif[:, t, :].unsqueeze(1).to_broadcast([P, GRP, TOPG]), ALU.is_equal))
                c.wait()
                c.add(V.tensor_reduce(gmask[:], geq[:], X, ALU.max))
                c.wait()
                c.add(TSC(gmm[:], gmask[:], 1.0, None, SU))
                tg = TS * GRP
                c.add(TT(msk[:].rearrange("p t (g m) -> p (t g) m", m=PER), sc[:].rearrange("p t (g m) -> p (t g) m", m=PER),
                         gmask[:].rearrange("p t g -> p (t g)").unsqueeze(2).to_broadcast([P, tg, PER]), M))
                c.wait()
                c.add(TT(msk[:].rearrange("p t (g m) -> p (t g) m", m=PER), msk[:].rearrange("p t (g m) -> p (t g) m", m=PER),
                         gmm[:].rearrange("p t g -> p (t g)").unsqueeze(2).to_broadcast([P, tg, PER]), AD))
                c.wait()
                for t in range(TS):
                    c.add(V.max(ev[:, t, :], msk[:, t, :]))
                c.wait()
                for t in range(TS):
                    c.add(V.max_index(ei[:, t, :], ev[:, t, :], msk[:, t, :]))
                c.add(V.tensor_reduce(wsum[:, 0, :], ev[:, :, 0:TOPK], X, AD))
                c.wait()
                c.add(V.tensor_copy(eif[:], ei[:, :, 0:TOPK]))
                c.add(V.reciprocal(wsum[:, 1, :], wsum[:, 0, :]))
                dve.wait_ge(s_dve, c.n - 1)
                c.add(TT(oh[:], iota_e[:].unsqueeze(1).to_broadcast([P, TS * TOPK, E]),
                         eif[:].rearrange("p t k -> p (t k)").unsqueeze(2).to_broadcast([P, TS * TOPK, E]), ALU.is_equal))
                c.wait()
                V.tensor_reduce(memb[:], oh[:].rearrange("p (t k) e -> p t e k", k=TOPK), X, ALU.max).then_inc(s_memb, 1)
                c.add(STT(PAY[b % 2][:, :, :, D + 1], ev[:, :, 0:TOPK], ROUTE_SCALE,
                          wsum[:, 1, :].unsqueeze(2).to_broadcast([P, TS, TOPK]), M, M))

            def places(b):
                dve.wait_ge(s_posp, b + 1)
                if b == 0:
                    c.add(V.tensor_copy(cb[:], cb0[:]))
                c.wait()
                c.add(TT(dpos[:], PS[:, 3, 0:TS * E].rearrange("p (t e) -> p t e", e=E),
                         cb[:].unsqueeze(1).to_broadcast([P, TS, E]), AD))
                c.wait()
                c.add(TT(cb[:], cb[:], PS[:, 3, TS * E:TS * E + E], AD))
                for t in range(TS):
                    c.add(TT(oh[:, t * TOPK:(t + 1) * TOPK, :], oh[:, t * TOPK:(t + 1) * TOPK, :],
                             dpos[:, t, :].unsqueeze(1).to_broadcast([P, TOPK, E]), M))
                c.wait()
                c.add(V.tensor_reduce(destf[:], oh[:], X, AD))
                c.wait()
                V.tensor_copy(dest[:, b % 2, :], destf[:]).then_inc(s_dest, 1)

            V.memset(cst[:, 0:1], math.pi / 2)
            V.memset(cst[:, 1:2], 1e-37)
            V.memset(cst[:, 2:3], EPS)
            V.memset(cst[:, 3:4], -LN2H)
            dve.wait_ge(s_chw, 16)
            TSC(ch[:, 3:4].bitcast(i32), chan_s[:, 4:5].bitcast(i32), 0x7FFFFFFF, None, ALU.bitwise_and).then_inc(s_spin, 1)
            TSC(ch[:, 0:1], chan_s[:, 5:6], 1.0 / (2 * math.pi), None, M)
            c.add(TSC(ch[:, 7:8], chan_s[:, 4:5], 0.0, None, ALU.max))
            ln1_stats(0)
            dve.wait_ge(s_spout, 1)
            c.add(TT(ch[:, 6:7], ch[:, 7:8], ch[:, 5:6], AD))
            c.wait()
            TSC(ch[:, 1:2], ch[:, 6:7], -8.0, None, M)
            TSC(ch[:, 2:3], ch[:, 6:7], -16.0, None, M).then_inc(s_chan, 1)
            ln1_stats(1)
            ln1_rows(0)
            ln1_stats(2)
            ln1_stats(3)
            dve.wait_ge(s_small, 48)
            TSC(w_out_n[:], w_out_s[:, 0, :], -1.0, None, M).then_inc(s_chan, 1)
            dve.wait_ge(s_const, 9)
            for stage, b in (
                    (ln1_rows, 1), (turns, 0), (ln1_rows, 2), (z_parts, 0), (z_sum, 0), (gate_input, 0),
                    (turns, 1), (rotate_back, 0), (scan_rotate, 0), (z_parts, 1), (z_sum, 1), (turns, 2), (residual1, 0),
                    (gate_input, 1), (ln1_rows, 3), (ln2_rows, 0), (rotate_back, 1), (scan_rotate, 1), (z_parts, 2), (choose, 0),
                    (z_sum, 2), (residual1, 1), (places, 0), (gate_input, 2), (ln2_rows, 1), (rotate_back, 2),
                    (scan_rotate, 2), (turns, 3), (choose, 1), (z_parts, 3), (places, 1), (z_sum, 3), (residual1, 2),
                    (gate_input, 3), (ln2_rows, 2), (rotate_back, 3), (scan_rotate, 3), (choose, 2),
                    (places, 2), (residual1, 3), (ln2_rows, 3), (choose, 3), (places, 3)):
                stage(b)

            CN, CBK, CUM, LE, TMP = 0, 1, 2, 3, 4
            c.add(TT(cnt[:, CN, :], cb[:], cb0[:], SU))
            c.wait()
            c.add(TT(cmpb, cnt[:, CN, :].unsqueeze(2).to_broadcast([P, E, NT]),
                     thr[:].unsqueeze(1).to_broadcast([P, E, NT]), ALU.is_gt))
            c.wait()
            c.add(V.tensor_reduce(cnt[:, CBK, :], cmpb, X, AD))
            c.wait()
            c.add(V.tensor_tensor_scan(cnt[:, CUM, :], cnt[:, CBK, :], zero_e[:], 0.0, AD, AD))
            c.wait()
            c.add(TSC(cnt[:, LE, :], cnt[:, CUM, :], iota_p[:, 0:1], None, ALU.is_le))
            c.wait()
            c.add(TT(cnt[:, TMP, :], cnt[:, LE, :], cnt[:, CBK, :], M))
            c.add(V.tensor_reduce(tabf[:, 0:1], cnt[:, LE, :], X, AD))
            c.wait()
            c.add(V.tensor_reduce(tabf[:, 1:2], cnt[:, TMP, :], X, AD))
            c.wait()
            c.add(TT(tabf[:, 1:2], iota_p[:], tabf[:, 1:2], SU))
            c.wait()
            c.add(TSC(tabf[:, 1:2], tabf[:, 1:2], float(P), None, M))
            c.wait()
            c.add(STT(tabf[:, 2:3], tabf[:, 0:1], float(CAP), tabf[:, 1:2], M, AD))
            c.wait()
            c.add(TSC(tabf[:, 2:3], tabf[:, 2:3], float(PADROW), None, ALU.min))
            c.add(TSC(tabf[:, 3:4], tabf[:, 0:1], float(E - 1), float(EW), ALU.min, M))
            c.wait()
            V.tensor_copy(tabs[0:1, 2 * P:2 * P + E], cb[0:1, :]).then_inc(s_tabf, 1)
            dve.wait_ge(s_tabp, 1)
            V.tensor_copy(tabs[0:1, 0:2 * P], PS[0:1, 0, 0:2 * P]).then_inc(s_tab, 1)

            def shared_hidden(b):
                dve.wait_ge(s_shs, b + 1)
                TT(SHG[:].rearrange("p (h n) -> p h n", h=KD), SHG[:].rearrange("p (h n) -> p h n", h=KD),
                   PS[:, 4:6, :], M).then_inc(s_shh, 1)

            def shared_out(b):
                dve.wait_ge(s_shyp, b + 1)
                TT(resid[:, tiles(b), :], resid[:, tiles(b), :],
                   PS[:, 6:8, :].rearrange("p a (c d) -> p (a c) d", d=D), AD).then_inc(s_resid, 1)

            for b in range(SHARED_BEFORE):
                shared_hidden(b)
                shared_out(b)

            def hidden(j, r, slot):
                dve.wait_ge(s_sg, j + 1)
                if not isinstance(j, int) or j >= 2:
                    dve.wait_ge(s_hp, j - 1)
                STT(hh[:, r, :], sg[:, r, :], xs[:, slot, D + 1:D + 2], PS[:, 2 + r, P:2 * P], M, M).then_inc(s_hh, 1)

            def block_out(j, r, slot, scattered):
                dve.wait_ge(s_yp, j + 1)
                if scattered is not None:
                    dve.wait_ge(s_ys[slot], scattered)
                V.tensor_copy(yy[:, slot, :], PS[:, 6 + r, 0:D]).then_inc(s_y, 1)

            def step(s, u):
                fixed = isinstance(s, int)
                if not fixed or 2 <= s <= BLOCKS + 1:
                    hidden(s - 2, u % 2, (u - 2) % NXS)
                if not fixed or 4 <= s:
                    j = s - 4
                    if fixed:
                        scattered = 16 * (j // NY) if j >= NY else None
                    else:
                        scattered = (s - u) * (16 // NY) + 16 * ((u - 4) // NY)
                    block_out(j, u % 2, (u - 4) % NY, scattered)

            for s in range(NXS):
                step(s, s)
            with dve.Fori(NXS, BLOCKS, NXS) as i:
                for u in range(NXS):
                    step(i + u, u)
            for s in range(BLOCKS, BLOCKS + 4):
                step(s, s)
            for b in range(SHARED_BEFORE, B):
                shared_hidden(b)
            for n in range(NT):
                if n >= SHARED_BEFORE * TS and n % TS == 0:
                    shared_out(n // TS)
                o = (n % NC) * TOPK * D
                dve.wait_ge(s_cin[n % NC], 16 * (n // NC + 1))
                c.add(TT(flat[:, o:o + 3 * D], flat[:, o:o + 3 * D], flat[:, o + 3 * D:o + 6 * D], AD))
                c.wait()
                c.add(TT(flat[:, o:o + D], flat[:, o:o + D], flat[:, o + D:o + 2 * D], AD))
                c.add(TT(flat[:, o + 2 * D:o + 3 * D], flat[:, o + 2 * D:o + 3 * D], resid[:, n, :], AD))
                c.wait()
                TT(resid[:, n, :], flat[:, o:o + D], flat[:, o + 2 * D:o + 3 * D], AD).then_inc(s_fin, 1)

        @block.tensor
        def _(pe):
            mm = nc.tensor.matmul

            def ln1_transpose(b):
                pe.wait_ge(s_xn, b + 1)
                at_least(pe, s_xnt, b)
                at_least(pe, s_xn2, b - 2)
                for t in range(TS):
                    for k in range(KD):
                        ins = nc.tensor.transpose(PS[:, k, t * P:(t + 1) * P], XN[:, t * D + k * P:t * D + (k + 1) * P], ident[:])
                ins.then_inc(s_xntp, 1)

            def project(b):
                pe.wait_ge(s_xnt, b + 1)
                at_least(pe, s_xh, 2 * b)
                at_least(pe, s_dest, b - 2)
                at_least(pe, s_sc, b - 2)
                for m in range(KD):
                    for k in range(KD):
                        ins = mm(PS[:, 2 + m, :], w_in_s[:, k, m * P:(m + 1) * P], XNT[:, k * SEQ:(k + 1) * SEQ],
                                 start=(k == 0), stop=(k == KD - 1))
                ins.then_inc(s_xhp, 1)

            def gate(b):
                pe.wait_ge(s_xh, 2 * b + 2)
                at_least(pe, s_gates, 2 * b)
                for g in range(2):
                    for k in range(KD):
                        ins = mm(PS[:, 4 + g, :], bd[:, g, k, :], XH[b % 2][:, k * SEQ:(k + 1) * SEQ],
                                 start=(k == 0), stop=(k == KD - 1))
                ins.then_inc(s_gp, 1)

            def ln2_transpose(b):
                pe.wait_ge(s_pay, b + 1)
                pe.wait_ge(s_xnt, min(b + 3, B))
                at_least(pe, s_xn2, b)
                for t in range(TS):
                    for k in range(KD):
                        ins = nc.tensor.transpose(PS[:, k, t * P:(t + 1) * P], PAY[b % 2][:, t, 0, k * P:(k + 1) * P], ident[:])
                ins.then_inc(s_xn2p, 1)

            def logits(b):
                pe.wait_ge(s_xn2, b + 1)
                pe.wait_ge(s_xh, 2 * min(b + 3, B))
                at_least(pe, s_sc, b)
                for t in range(TS):
                    for k in range(KD):
                        ins = mm(PS[:, 2, t * E:(t + 1) * E], XN2T[:, b, k, t * P:(t + 1) * P], gwt_s[:, k, :],
                                 start=(k == 0), stop=(k == KD - 1))
                ins.then_inc(s_lgp, 1)

            def out_project(b):
                pe.wait_ge(s_prod, b + 1)
                at_least(pe, s_x1, b)
                parts = ((T[1], w_out_s[:, 0, :]), (T[2], w_out_n[:]), (T[4], w_out_s[:, 1, :]), (T[5], w_out_s[:, 1, :]))
                for t in range(TS):
                    for n, (h, w) in enumerate(parts):
                        ins = mm(PS[:, 6 + t // 2, (t % 2) * D:(t % 2 + 1) * D], h[:, t * P:(t + 1) * P], w,
                                 start=(n == 0), stop=(n == len(parts) - 1))
                ins.then_inc(s_outp, 1)

            def positions(b):
                pe.wait_ge(s_memb, b + 1)
                at_least(pe, s_dest, b)
                for t in range(TS):
                    for v in range(t + 1):
                        mm(PS[:, 3, t * E:(t + 1) * E], (tri if v == t else ones)[:], memb[:, v, :], start=(v == 0), stop=(v == t))
                for v in range(TS):
                    ins = mm(PS[:, 3, TS * E:TS * E + E], ones[:], memb[:, v, :], start=(v == 0), stop=(v == TS - 1))
                ins.then_inc(s_posp, 1)

            pe.wait_ge(s_const, 1)
            pe.wait_ge(s_win, 16)
            ln1_transpose(0)
            project(0)
            ln1_transpose(1)
            pe.wait_ge(s_gatew, 16)
            gate(0)
            project(1)
            gate(1)
            pe.wait_ge(s_const, 9)
            pe.wait_ge(s_small, 48)
            pe.wait_ge(s_chan, 2)
            for stage, b in (
                    (ln1_transpose, 2), (project, 2), (gate, 2), (out_project, 0), (ln2_transpose, 0), (logits, 0),
                    (out_project, 1), (ln1_transpose, 3), (positions, 0), (project, 3), (ln2_transpose, 1), (gate, 3), (logits, 1),
                    (out_project, 2), (positions, 1), (ln2_transpose, 2), (logits, 2),
                    (out_project, 3), (positions, 2), (ln2_transpose, 3), (logits, 3), (positions, 3)):
                stage(b)
            pe.wait_ge(s_tabf, 1)
            mm(PS[0:1, 0, 0:P], tabf[:, 2:3], ident[:], start=True, stop=True)
            mm(PS[0:1, 0, P:2 * P], tabf[:, 3:4], ident[:], start=True, stop=True).then_inc(s_tabp, 1)

            def shared(b):
                pe.wait_ge(s_dest, B)
                at_least(pe, s_shh, b)
                for h in range(KD):
                    for g in range(2):
                        for k in range(KD):
                            ins = mm(PS[:, 2 + 2 * g + h, :], sw13_s[:, k, g, h * P:(h + 1) * P], XN2T[:, b, k, :],
                                     start=(k == 0), stop=(k == KD - 1))
                ins.then_inc(s_shgp, 1)
                pe.wait_ge(s_shh, b + 1)
                at_least(pe, s_resid, b)
                for t in range(TS):
                    for h in range(KD):
                        ins = mm(PS[:, 6 + t // 2, (t % 2) * D:(t % 2 + 1) * D], SHG[:, h * SEQ + t * P:h * SEQ + (t + 1) * P],
                                 sw2_s[:, h, :], start=(h == 0), stop=(h == KD - 1))
                ins.then_inc(s_shyp, 1)

            pe.wait_ge(s_shw, 32)
            for b in range(SHARED_BEFORE):
                shared(b)
            pe.wait_ge(s_resid, SHARED_BEFORE)
            pe.wait_ge(s_tab, 1)
            pe.wait_ge(s_wearly, 16)
            pe.wait_ge(s_wlate, 16)

            def expert_of(j):
                return pe.value_load(tabs[0:1, bass.ds(j + P, 1)], min_val=0, max_val=(E - 1) * EW)

            def rows_t(j, r, slot, loads):
                pe.wait_ge(s_xs[slot], loads)
                if not isinstance(j, int) or j >= 2:
                    pe.wait_ge(s_xt, j - 1)
                for k in range(KD):
                    ins = nc.tensor.transpose(PS[:, r, k * P:(k + 1) * P], xs[:, slot, k * P:(k + 1) * P], ident[:])
                ins.then_inc(s_xtp, 1)

            def gate_up(j, r):
                w = expert_of(j)
                pe.wait_ge(s_xt, j + 1)
                if not isinstance(j, int) or j >= 2:
                    pe.wait_ge(s_hh, j - 1)
                for k in range(KD):
                    ins = mm(PS[:, 2 + r, 0:2 * P], xT[:, r, k * P:(k + 1) * P], W[:, bass.ds(w + k * 2 * P, 2 * P)],
                             start=(k == 0), stop=(k == KD - 1))
                ins.then_inc(s_gup, 1)

            def hidden_t(j, r):
                pe.wait_ge(s_hh, j + 1)
                if not isinstance(j, int) or j >= 2:
                    pe.wait_ge(s_ht, j - 1)
                nc.tensor.transpose(PS[:, 4 + r, 0:P], hh[:, r, :], ident[:]).then_inc(s_hp, 1)

            def down(j, r):
                w = expert_of(j)
                pe.wait_ge(s_ht, j + 1)
                if not isinstance(j, int) or j >= 2:
                    pe.wait_ge(s_y, j - 1)
                mm(PS[:, 6 + r, 0:D], hT[:, r, :], W[:, bass.ds(w + KD * 2 * P, D)], start=True, stop=True).then_inc(s_yp, 1)

            def step(s, u):
                fixed = isinstance(s, int)
                if not fixed or 2 <= s <= BLOCKS + 1:
                    gate_up(s - 2, u % 2)
                if not fixed or 4 <= s:
                    down(s - 4, u % 2)
                if not fixed or 3 <= s <= BLOCKS + 2:
                    hidden_t(s - 3, (u - 3) % 2)
                if not fixed or s < BLOCKS:
                    loads = 16 * (s // NXS + 1) if fixed else (s - u) * (16 // NXS) + 16
                    rows_t(s, u % 2, u % NXS, loads)

            for s in range(NXS):
                step(s, s)
            with pe.Fori(NXS, BLOCKS, NXS) as i:
                for u in range(NXS):
                    step(i + u, u)
            for s in range(BLOCKS, BLOCKS + 4):
                step(s, s)
            pe.wait_ge(s_y, BLOCKS)
            for b in range(SHARED_BEFORE, B):
                shared(b)


_LAUNCH = ["x", "chan", "w_in", "gate_bd", "w_out", "b_out", "gate_wt", "experts", "sw13", "sw2"]


def kernel(**inputs):
    import numpy as _np
    import concourse.bacc as _bacc
    from concourse import mybir as _mybir
    from concourse.bass_utils import run_bass_kernel_spmd as _run

    a = {k: _np.asarray(v) for k, v in inputs.items()}
    P = 128
    chan = _np.stack([a["L0_attn_b_in"][:P], a["L0_attn_b_in"][P:], a["L0_attn_b_gx"].reshape(P), a["L0_attn_b_ga"].reshape(P),
                      a["L0_attn_a_real"], a["L0_attn_a_imag"]], axis=1)
    E, F, D = a["L0_ffn_w11"].shape
    K = D // P
    w13 = _np.stack([a["L0_ffn_w11"], a["L0_ffn_w33"]])
    w13 = w13.reshape(2, E, F, K, P).transpose(4, 1, 3, 0, 2).reshape(P, E, K * 2 * F)
    w2 = a["L0_ffn_w22"].transpose(2, 0, 1)
    sw13 = _np.stack([a["L0_ffn_sw1"], a["L0_ffn_sw3"]])
    sw13 = sw13.reshape(2, sw13.shape[1], K, P).transpose(3, 2, 0, 1)
    sw2 = a["L0_ffn_sw2"].T.reshape(K, P, D).transpose(1, 0, 2)
    H, GI, GO = a["L0_attn_W_gx"].shape
    bd = _np.zeros((P, 2, K, P), a["L0_attn_W_gx"].dtype)
    for g, name in enumerate(("L0_attn_W_gx", "L0_attn_W_ga")):
        for h in range(H):
            k, r = divmod(h * GI, P)
            bd[r:r + GI, g, k, h * GO:(h + 1) * GO] = a[name][h]
    laid = dict(x=a["L0_attn_x"], chan=chan, w_in=a["L0_attn_W_in"], gate_bd=bd,
                w_out=a["L0_attn_W_out"], b_out=a["L0_attn_b_out"],
                gate_wt=a["L0_ffn_gate_w"].T.reshape(K, P, E).transpose(1, 0, 2),
                experts=_np.concatenate([w13, w2], axis=2), sw13=sw13, sw2=sw2)
    nc = _bacc.Bacc("TRN2", target_bir_lowering=False, num_devices=1)
    arrays, args = {}, []
    for name in _LAUNCH:
        v = _np.ascontiguousarray(laid[name])
        arrays[f"in_{name}"] = v
        args.append(nc.dram_tensor(f"in_{name}", v.shape, _mybir.dt.from_np(v.dtype), kind="ExternalInput").ap())
    shape = a["L0_attn_x"].shape
    args.append(nc.dram_tensor("out_0", shape, _mybir.dt.float32, kind="ExternalOutput").ap())
    preln_recurrence_moe(nc, *args)
    r = _run(nc, [arrays], core_ids=[0])
    return r.results[0]["out_0"]
```

```python
import concourse.bass as bass
from concourse import mybir
from concourse.alu_op_type import AluOpType as ALU
from contextlib import ExitStack
import math


def preln_recurrence_moe(nc, x, chan, w_in, gate_bd, w_out, b_out, gate_wt, experts, sw13, sw2, out):
    f32 = mybir.dt.float32
    bf16 = mybir.dt.bfloat16
    i32 = mybir.dt.int32
    u32 = mybir.dt.uint32
    ACT = mybir.ActivationFunctionType
    X = mybir.AxisListType.X

    B, SEQ, D = x.shape
    N = B * SEQ
    P = 128
    KD = D // P
    TS = SEQ // P
    NT = N // P
    E, GRP, TOPG, TOPK = 32, 8, 4, 6
    PER = E // GRP
    ROUTE_SCALE = 2.5
    EPS = 1e-5
    CAP = N + P
    PADROW = E * CAP
    ROW = D + 2
    BLOCKS = N * TOPK // P + E
    EW = KD * 2 * P + D
    SHARED_BEFORE = B // 2
    ACT_PADS = 12
    NXS = 8
    NY = 4
    SKIP = 1 << 20
    MAGIC = 1.5 * 2.0 ** 23
    TWO_PI = 6.283185
    LN2H = 0.5 * math.log(2.0)

    xt_d = x.rearrange("b (t p) d -> b p t d", p=P)
    out_d = out.rearrange("b (t p) d -> (b t) p d", p=P)
    bucket = nc.dram_tensor("bucket_rows", (E * CAP + P, ROW), f32)
    choice = nc.dram_tensor("choice_rows", (N * TOPK, D), f32)
    bucket_ap = bucket.ap()
    choice_ap = choice.ap()
    choice_t = choice_ap.rearrange("(n p k) d -> n p (k d)", p=P, k=TOPK)

    ctx = ExitStack()
    with ctx:
        def sb(name, shape, dt=f32):
            return ctx.enter_context(nc.sbuf_tensor(name, shape, dt))

        def sem(name):
            return ctx.enter_context(nc.semaphore(name))

        W = sb("expert_weights", [P, E * EW])
        UNITS = 40
        EARLY = (E * EW - UNITS * SEQ) // EW
        base = E * EW - UNITS * SEQ

        def unit(u, k=1):
            return W[:, base + u * SEQ: base + (u + k) * SEQ]

        XH = [unit(0, 2), unit(2, 2)]
        SN = [unit(4, 2), unit(6, 2)]
        CS = [unit(8, 2), unit(10, 2)]
        GX = [unit(12), unit(13)]
        RHO = [unit(14), unit(15)]
        T = [unit(16 + i) for i in range(8)]
        XNT = unit(24, 2)
        FR = unit(26, 2)
        XN = unit(28, 2)
        AB = sb("turn_abs", [P, 2 * SEQ])
        TURN = unit(30, 2)
        RHO2 = unit(32)
        GU = unit(33)
        E2 = GU
        Q = unit(34)
        W1 = unit(35)
        ZR = unit(36)
        M2 = unit(37)
        SR = unit(38)
        RR = unit(39)

        resid = sb("resid", [P, NT, D])
        XN2T = sb("xn2_t", [P, B, KD, SEQ])
        PAYS = sb("payload", [P, 2 * TS, TOPK, ROW])
        PAY = [PAYS[:, 0:TS, :, :], PAYS[:, TS:2 * TS, :, :]]
        PADT = sb("pad_rows", [P, ROW])
        w_in_s = sb("w_in_s", [P, KD, D])
        w_out_s = sb("w_out_s", [P, KD, D])
        w_out_n = sb("w_out_n", [P, D])
        bd = sb("gate_blockdiag", [P, 2, KD, P])
        sw13_s = sb("sw13_s", [P, KD, 2, D])
        sw2_s = sb("sw2_s", [P, KD, D])
        gwt_s = sb("gwt_s", [P, KD, E])
        bout_s = sb("bout_s", [P, D])
        chan_s = sb("chan_s", [P, 6])
        ident = sb("ident", [P, P])
        tri = sb("tri", [P, P], bf16)
        ones = sb("ones", [P, P], bf16)
        iota_g = sb("iota_g", [P, GRP])
        iota_e = sb("iota_e", [P, E])
        iota_p = sb("iota_p", [P, 1])
        thr = sb("thr", [P, NT])
        cb0 = sb("bucket_base", [P, E])
        cb = sb("bucket_next", [P, E])
        cst = sb("consts", [P, 4])
        ch = sb("chan_derived", [P, 10])
        st1 = sb("st1", [P, B, TS, 6])
        st2 = sb("st2", [P, B, TS, 6])
        mv1 = sb("mv1", [P, B, TS, 2])
        rs1 = sb("rs1", [P, B, 2, TS])
        mv2 = sb("mv2", [P, B, TS, 2])
        rs2 = sb("rs2", [P, B, 2, TS])
        sc = sb("scores", [P, TS, E])
        sc2 = sb("scores_tmp", [P, TS, E])
        gm = sb("group_max", [P, TS, GRP])
        gv = sb("gv", [P, TS, 8])
        gi = sb("gi", [P, TS, 8], u32)
        gif = sb("gif", [P, TS, TOPG])
        geq = sb("geq", [P, TS, GRP, TOPG])
        gmask = sb("gmask", [P, TS, GRP])
        gmm = sb("gmm", [P, TS, GRP])
        msk = sb("masked", [P, TS, E])
        ev = sb("ev", [P, TS, 8])
        ei = sb("ei", [P, TS, 8], u32)
        eif = sb("eif", [P, TS, TOPK])
        wsum = sb("wsum", [P, 2, TS])
        oh = sb("one_hot", [P, TS * TOPK, E])
        memb = sb("member", [P, TS, E], bf16)
        dpos = sb("dpos", [P, TS, E])
        dest = sb("dest", [P, 2, TS * TOPK], i32)
        destf = sb("destf", [P, TS * TOPK])
        cnt = sb("cnt", [P, 6, E])
        zero_e = sb("zero_e", [P, E])
        cmpb = oh[:].rearrange("p q e -> p (q e)")[:, 0:E * NT].rearrange("p (e n) -> p e n", n=NT)
        tabf = sb("tabf", [P, 4])
        tabs = sb("tabs", [1, 2 * P + E], i32)
        at = [TS * TOPK * ROW]
        flat = PAYS[:, :, :, :].rearrange("p t k r -> p (t k r)")

        def over_payload(n, w):
            at[0] += n * w
            return flat[:, at[0] - n * w:at[0]].rearrange("p (n w) -> p n w", w=w)

        xs = over_payload(NXS, ROW)
        xT = over_payload(2, D)
        sg = over_payload(2, P)
        hh = over_payload(2, P)
        hT = over_payload(2, P)
        yy = over_payload(NY, D)
        xs_idx = xs.bitcast(i32)
        NC = 2 * TS * TOPK * ROW // (TOPK * D)
        SHG = AB

        PS = ctx.enter_context(nc.psum_tensor("PS", [P, 8, 512], f32))

        s_x = [sem(f"x_loaded{b}") for b in range(B)]
        s_win = sem("w_in_loaded")
        s_chw = sem("channel_vectors_loaded")
        s_gatew = sem("gate_weights_loaded")
        s_small = sem("small_weights_loaded")
        s_shw = sem("shared_weights_loaded")
        s_wearly = sem("early_experts_loaded")
        s_wlate = sem("late_experts_loaded")
        s_const = sem("constants_built")
        s_bout = sem("output_bias_added")
        s_dve = sem("dve_chain")
        s_act = sem("act_chain")
        s_pool = sem("pool_chain")
        s_spin = sem("softplus_input")
        s_spout = sem("softplus_log")
        s_chan = sem("channel_constants")
        s_stats1 = sem("ln1_stats")
        s_rstd1 = sem("ln1_rstd")
        s_xn = sem("ln1_rows")
        s_xntp = sem("ln1_transposed_psum")
        s_xnt = sem("ln1_transposed")
        s_xhp = sem("projected_psum")
        s_xh = sem("projected")
        s_gp = sem("gates_psum")
        s_gates = sem("gates")
        s_rho = sem("decay_ready")
        s_step = sem("step_angles")
        s_turn = sem("turns_reduced")
        s_trig = sem("sines_ready")
        s_m2 = sem("z_squared_abs")
        s_zabs = sem("z_abs_ready")
        s_zt = sem("z_abs_plus_re")
        s_zroot = sem("z_root_ready")
        s_xused = sem("projection_used")
        s_prod = sem("rotated_products")
        s_outp = sem("attention_out_psum")
        s_x1 = sem("first_residual")
        s_stats2 = sem("ln2_stats")
        s_rstd2 = sem("ln2_rstd")
        s_pay = sem("ln2_rows")
        s_xn2p = sem("ln2_transposed_psum")
        s_xn2 = sem("ln2_transposed")
        s_lgp = sem("router_logits_psum")
        s_sc = sem("router_scores")
        s_memb = sem("membership")
        s_posp = sem("positions_psum")
        s_dest = sem("bucket_rows_known")
        s_rep = sem("ln2_rows_repeated")
        s_rowid = sem("output_row_ids")
        s_scat = [sem(f"rows_scattered{b}") for b in range(B)]
        s_padrow = sem("padding_rows_known")
        s_tabf = sem("block_table_columns")
        s_tabp = sem("block_table_psum")
        s_tab = sem("block_table")
        s_padt = sem("padding_tile")
        s_pad = sem("padding_written")
        s_shgp = sem("shared_gate_up_psum")
        s_shs = sem("shared_silu")
        s_shh = sem("shared_hidden")
        s_shyp = sem("shared_out_psum")
        s_resid = sem("second_residual")
        s_xs = [sem(f"block_rows{i}") for i in range(NXS)]
        s_xtp = sem("block_transposed_psum")
        s_xt = sem("block_transposed")
        s_gup = sem("block_gate_up_psum")
        s_sg = sem("block_silu")
        s_hh = sem("block_hidden")
        s_hp = sem("hidden_transposed_psum")
        s_ht = sem("hidden_transposed")
        s_yp = sem("block_out_psum")
        s_y = sem("block_out")
        s_ys = [sem(f"block_scattered{i}") for i in range(NY)]
        s_cin = [sem(f"choices_loaded{i}") for i in range(NC)]
        s_fin = sem("token_tile_summed")
        s_fin_pool = sem("token_tile_summed_pool")
        s_out = [sem(f"token_stored{i}") for i in range(4)]

        block = ctx.enter_context(nc.Block())

        class Chain:

            def __init__(self, eng, s):
                self.eng, self.s, self.n = eng, s, 0

            def add(self, ins):
                ins.then_inc(self.s, 1)
                self.n += 1

            def wait(self):
                self.eng.wait_ge(self.s, self.n)

        def at_least(eng, s, n):
            if n > 0:
                eng.wait_ge(s, n)

        def tiles(b):
            return slice(b * TS, (b + 1) * TS)

        def pad_buckets(eng, which):
            for e in which:
                row = eng.value_load(tabs[0:1, 2 * P + e:2 * P + e + 1], min_val=0, max_val=E * CAP)
                eng.dma_start(bucket_ap[bass.ds(row, P), :], PADT[:]).then_inc(s_pad, 16)

        def pool_sums(n):
            return n % 4 == 2

        def summed(eng, n):
            if pool_sums(n):
                eng.wait_ge(s_fin_pool, n // 4 + 1)
            else:
                eng.wait_ge(s_fin, n + 1 - (n + 2) // 4)

        def sum_rows(eng, api, chain, n):
            add, o = api.tensor_tensor, (n % NC) * TOPK * D
            eng.wait_ge(s_cin[n % NC], 16 * (n // NC + 1))
            chain.add(add(flat[:, o:o + 3 * D], flat[:, o:o + 3 * D], flat[:, o + 3 * D:o + 6 * D], ALU.add))
            chain.wait()
            chain.add(add(flat[:, o:o + D], flat[:, o:o + D], flat[:, o + D:o + 2 * D], ALU.add))
            chain.add(add(flat[:, o + 2 * D:o + 3 * D], flat[:, o + 2 * D:o + 3 * D], resid[:, n, :], ALU.add))
            chain.wait()
            add(resid[:, n, :], flat[:, o:o + D], flat[:, o + 2 * D:o + 3 * D],
                ALU.add).then_inc(s_fin_pool if pool_sums(n) else s_fin, 1)

        @block.sync
        def _(sp):
            for b in range(B):
                sp.dma_start(resid[:, tiles(b), :], xt_d[b]).then_inc(s_x[b], 16)
                if b == 0:
                    sp.dma_start(w_in_s[:], w_in.rearrange("(k p) n -> p k n", p=P)).then_inc(s_win, 16)
            sp.dma_start(W[:, 0:EARLY * EW].rearrange("p (e w) -> p e w", w=EW), experts[:, 0:EARLY, :]).then_inc(s_wearly, 16)
            sp.dma_start(sw13_s[:], sw13).then_inc(s_shw, 16)
            sp.dma_start(sw2_s[:], sw2).then_inc(s_shw, 16)
            sp.wait_ge(s_padt, 3)
            sp.dma_start(bucket_ap[PADROW:PADROW + P, :], PADT[:]).then_inc(s_pad, 16)
            sp.wait_ge(s_outp, B)
            sp.wait_ge(s_prod, B)
            sp.wait_ge(s_zroot, B)
            sp.dma_start(W[:, EARLY * EW:].rearrange("p (e w) -> p e w", w=EW), experts[:, EARLY:, :]).then_inc(s_wlate, 16)
            sp.wait_ge(s_padrow, 1)
            pad_buckets(sp, range(ACT_PADS, E))
            sp.wait_ge(s_tab, 1)
            sp.wait_ge(s_pad, 16 * (E + 1))
            for b in range(B):
                sp.wait_ge(s_scat[b], 16 * TS * TOPK)

            def load_block(j, slot, tail_rounds):
                if tail_rounds is not None:
                    sp.wait_ge(s_ys[slot % NY], tail_rounds)
                row = sp.value_load(tabs[0:1, bass.ds(j, 1)], min_val=0, max_val=E * CAP)
                sp.dma_start(xs[:, slot, :], bucket_ap[bass.ds(row, P), :]).then_inc(s_xs[slot], 16)

            for j in range(NXS):
                load_block(j, j, None)
            with sp.Fori(NXS, BLOCKS, NXS) as i:
                for u in range(NXS):
                    load_block(i + u, u, (i - NXS) * (16 // NY) + 16 * (u // NY + 1))
            for q in range(NY):
                sp.wait_ge(s_ys[q], 16 * (BLOCKS // NY))
            for n in range(NT):
                if n >= NC:
                    summed(sp, n - NC)
                sp.dma_start(flat[:, (n % NC) * TOPK * D:(n % NC + 1) * TOPK * D], choice_t[n]).then_inc(s_cin[n % NC], 16)

        @block.gpsimd
        def _(pool):
            pch = Chain(pool, s_pool)
            pch.add(nc.gpsimd.memset(ident[:], 0.0))
            pch.add(nc.gpsimd.memset(tri[:], 1.0))
            pch.wait()
            nc.gpsimd.affine_select(out=ident[:], in_=ident[:], compare_op=ALU.not_equal, fill=1.0, base=0,
                                    pattern=[[-1, P]], channel_multiplier=1).then_inc(s_const, 1)
            nc.gpsimd.affine_select(out=tri[:], in_=tri[:], compare_op=ALU.is_gt, fill=0.0, base=0,
                                    pattern=[[1, P]], channel_multiplier=-1).then_inc(s_const, 1)
            nc.gpsimd.memset(ones[:], 1.0).then_inc(s_const, 1)
            nc.gpsimd.iota(iota_g[:], pattern=[[1, GRP]], base=0, channel_multiplier=0,
                           allow_small_or_imprecise_dtypes=True).then_inc(s_const, 1)
            nc.gpsimd.iota(iota_e[:], pattern=[[1, E]], base=0, channel_multiplier=0,
                           allow_small_or_imprecise_dtypes=True).then_inc(s_const, 1)
            nc.gpsimd.iota(iota_p[:], pattern=[[0, 1]], base=0, channel_multiplier=1,
                           allow_small_or_imprecise_dtypes=True).then_inc(s_const, 1)
            nc.gpsimd.iota(thr[:], pattern=[[P, NT]], base=0, channel_multiplier=0,
                           allow_small_or_imprecise_dtypes=True).then_inc(s_const, 1)
            nc.gpsimd.iota(cb0[:], pattern=[[CAP, E]], base=0, channel_multiplier=0,
                           allow_small_or_imprecise_dtypes=True).then_inc(s_const, 1)
            nc.gpsimd.memset(zero_e[:], 0.0).then_inc(s_const, 1)
            nc.gpsimd.memset(PADT[:, 0:D], 0.0).then_inc(s_padt, 1)
            nc.gpsimd.memset(PADT[:, D + 1:D + 2], 0.0).then_inc(s_padt, 1)
            nc.gpsimd.iota(PADT[:, D:D + 1].bitcast(i32), pattern=[[0, 1]], base=SKIP,
                           channel_multiplier=0).then_inc(s_padt, 1)
            pool.wait_ge(s_small, 48)
            for b in range(B):
                pool.wait_ge(s_xn, b + 1)
                nc.gpsimd.tensor_tensor(resid[:, tiles(b), :], resid[:, tiles(b), :],
                                        bout_s[:].unsqueeze(1).to_broadcast([P, TS, D]), ALU.add).then_inc(s_bout, 1)

            def row_ids(b):
                if b >= 2:
                    pool.wait_ge(s_scat[b - 2], 16 * TS * TOPK)
                nc.gpsimd.iota(PAY[b % 2].bitcast(i32)[:, :, :, D], pattern=[[P * TOPK, TS], [1, TOPK]], base=b * SEQ * TOPK,
                               channel_multiplier=TOPK).then_inc(s_rowid, 1)

            def scatter_rows(b):
                pool.wait_ge(s_rowid, b + 1)
                pool.wait_ge(s_rep, b + 1)
                pool.wait_ge(s_dest, b + 1)
                for t in range(TS):
                    for k in range(TOPK):
                        q = t * TOPK + k
                        nc.gpsimd.indirect_dma_start(
                            out=bucket_ap[:, :], out_offset=bass.IndirectOffsetOnAxis(ap=dest[:, b % 2, q:q + 1], axis=0),
                            in_=PAY[b % 2][:, t, k, :], in_offset=None).then_inc(s_scat[b], 16)

            row_ids(0)
            row_ids(1)
            scatter_rows(0)
            for b in range(1, B):
                scatter_rows(b)
                if b + 1 < B:
                    row_ids(b + 1)

            zero, last, last_row = (pool.alloc_register(n) for n in ("row_zero", "row_last", "row_bound"))
            pool.reg_mov(zero, 0)
            pool.reg_mov(last, N * TOPK - 1)

            def scatter(j, slot, ready):
                pool.wait_ge(s_y, ready)
                pool.reg_add(last_row, zero, last)
                nc.gpsimd.indirect_dma_start(
                    out=choice_ap[:, :], out_offset=bass.IndirectOffsetOnAxis(ap=xs_idx[:, slot, D:D + 1], axis=0),
                    in_=yy[:, slot % NY, :], in_offset=None,
                    bounds_check=last_row, oob_is_err=False).then_inc(s_ys[slot % NY], 16)

            with pool.Fori(0, BLOCKS, NXS) as i:
                for u in range(NXS):
                    scatter(i + u, u, i + u + 1)
            for n in range(NT):
                if pool_sums(n):
                    pool.wait_ge(s_resid, n // TS + 1)
                    sum_rows(pool, nc.gpsimd, pch, n)

        @block.scalar
        def _(act):
            ach = Chain(act, s_act)
            A = nc.scalar.activation

            tables = nc.scalar.preload_act_table_set
            EXP_LN, SILU = "natural_log_exp_and_others", "silu_and_others"

            def rstd(mv, rs, s_in, s_out, b):
                act.wait_ge(s_in, b + 1)
                ach.add(A(rs[:, b, 0, :], mv[:, b, :, 1], ACT.Ln, bias=cst[:, 2:3]))
                ach.wait()
                A(rs[:, b, 1, :], rs[:, b, 0, :], ACT.Exp, scale=-0.5).then_inc(s_out, 1)

            def rstd1(b):
                rstd(mv1, rs1, s_stats1, s_rstd1, b)

            def rstd2(b):
                rstd(mv2, rs2, s_stats2, s_rstd2, b)

            def ln1_transposed(b):
                act.wait_ge(s_xntp, b + 1)
                at_least(act, s_xhp, b)
                A(XNT, PS[:, 0:2, :], ACT.Copy).then_inc(s_xnt, 1)

            def projected(b):
                p = b % 2
                act.wait_ge(s_xhp, b + 1)
                at_least(act, s_xused, b - 1)
                for k in range(KD):
                    A(XH[p][:, k * SEQ:(k + 1) * SEQ], PS[:, 2 + k, :], ACT.Identity,
                      bias=chan_s[:, k:k + 1]).then_inc(s_xh, 1)

            def gates(b):
                p = b % 2
                act.wait_ge(s_gp, b + 1)
                A(GX[p], PS[:, 4, :], ACT.Sigmoid, bias=chan_s[:, 2:3]).then_inc(s_gates, 1)
                at_least(act, s_m2, b)
                A(GU, PS[:, 5, :], ACT.Sigmoid, bias=chan_s[:, 3:4]).then_inc(s_gates, 1)

            def step_turns(b):
                act.wait_ge(s_gates, 2 * b + 2)
                at_least(act, s_turn, b)
                if b == 0:
                    act.wait_ge(s_chan, 1)
                A(TURN[:, 0:SEQ], GU, ACT.Copy, scale=ch[:, 0:1]).then_inc(s_step, 1)

            def decay(b):
                p = b % 2
                act.wait_ge(s_gates, 2 * b + 2)
                at_least(act, s_prod, b - 1)
                at_least(act, s_m2, b)
                if b == 0:
                    act.wait_ge(s_chan, 1)
                A(RHO[p], GU, ACT.Exp, scale=ch[:, 1:2]).then_inc(s_rho, 1)
                ach.add(A(RHO2, GU, ACT.Exp, scale=ch[:, 2:3]))
                ach.wait()
                A(E2, RHO2, ACT.Square, scale=-1.0, bias=1.0).then_inc(s_rho, 1)

            def sines(b):
                p = b % 2
                act.wait_ge(s_turn, b + 1)
                A(SN[p], FR, ACT.Sin, scale=-TWO_PI)
                A(CS[p], AB[:], ACT.Sin, scale=-TWO_PI, bias=cst[:, 0:1]).then_inc(s_trig, 1)

            def zabs(b):
                act.wait_ge(s_m2, b + 1)
                ach.add(A(M2, M2, ACT.Ln, bias=cst[:, 1:2]))
                ach.wait()
                A(M2, M2, ACT.Exp, scale=0.5).then_inc(s_zabs, 1)

            def zroots(b):
                act.wait_ge(s_zt, b + 1)
                ach.add(A(M2, M2, ACT.Ln))
                ach.wait()
                A(SR, M2, ACT.Exp, scale=0.5, bias=cst[:, 3:4])
                A(RR, M2, ACT.Exp, scale=-0.5, bias=cst[:, 3:4]).then_inc(s_zroot, 1)

            def ln2_transposed(b):
                act.wait_ge(s_xn2p, b + 1)
                A(XN2T[:, b, :, :], PS[:, 0:2, :], ACT.Copy).then_inc(s_xn2, 1)

            def repeat_rows(b):
                act.wait_ge(s_pay, b + 1)
                for t in range(TS):
                    ins = A(PAY[b % 2][:, t, 1:TOPK, 0:D],
                            PAY[b % 2][:, t, 0, 0:D].unsqueeze(1).to_broadcast([P, TOPK - 1, D]), ACT.Copy)
                ins.then_inc(s_rep, 1)

            def scores(b):
                act.wait_ge(s_lgp, b + 1)
                at_least(act, s_memb, b)
                ach.add(A(sc2[:], PS[:, 2, 0:TS * E].rearrange("p (t e) -> p t e", e=E), ACT.Exp, scale=-1.0))
                ach.wait()
                ach.add(A(sc2[:], sc2[:], ACT.Ln, bias=1.0))
                ach.wait()
                A(sc[:, :, :], sc2[:], ACT.Exp, scale=-1.0).then_inc(s_sc, 1)

            act.dma_start(chan_s[:], chan).then_inc(s_chw, 16)
            act.dma_start(bd[:], gate_bd).then_inc(s_gatew, 16)
            act.dma_start(bout_s[:], b_out.partition_broadcast(P)).then_inc(s_small, 16)
            act.dma_start(w_out_s[:], w_out.rearrange("(k p) n -> p k n", p=P)).then_inc(s_small, 16)
            act.dma_start(gwt_s[:], gate_wt).then_inc(s_small, 16)
            tables(EXP_LN)
            act.wait_ge(s_spin, 1)
            ach.add(A(ch[:, 4:5], ch[:, 3:4], ACT.Exp, scale=-1.0))
            ach.wait()
            A(ch[:, 5:6], ch[:, 4:5], ACT.Ln, bias=1.0).then_inc(s_spout, 1)
            for stage, b in (
                    (rstd1, 0), (ln1_transposed, 0), (rstd1, 1), (rstd1, 2), (projected, 0), (ln1_transposed, 1),
                    (rstd1, 3), (gates, 0), (step_turns, 0), (tables, EXP_LN), (decay, 0), (projected, 1), (sines, 0),
                    (gates, 1), (step_turns, 1), (tables, EXP_LN), (zabs, 0), (decay, 1), (zroots, 0), (ln1_transposed, 2),
                    (sines, 1), (projected, 2), (gates, 2), (step_turns, 2), (tables, EXP_LN), (decay, 2), (zabs, 1),
                    (zroots, 1), (sines, 2), (tables, EXP_LN), (rstd2, 0), (ln2_transposed, 0), (scores, 0),
                    (repeat_rows, 0), (zabs, 2), (zroots, 2), (rstd2, 1), (ln1_transposed, 3), (projected, 3), (gates, 3),
                    (step_turns, 3), (ln2_transposed, 1), (tables, EXP_LN), (scores, 1), (decay, 3), (sines, 3),
                    (tables, EXP_LN), (zabs, 3), (zroots, 3), (repeat_rows, 1), (rstd2, 2), (ln2_transposed, 2),
                    (repeat_rows, 2), (scores, 2), (rstd2, 3), (ln2_transposed, 3), (scores, 3), (repeat_rows, 3)):
                stage(b)

            def shared(b):
                act.wait_ge(s_shgp, b + 1)
                at_least(act, s_shyp, b)
                A(SHG[:].rearrange("p (h n) -> p h n", h=KD), PS[:, 2:4, :], ACT.Silu).then_inc(s_shs, 1)

            def silu(j, r):
                act.wait_ge(s_gup, j + 1)
                A(sg[:, r, :], PS[:, 2 + r, 0:P], ACT.Silu).then_inc(s_sg, 1)

            def hidden_t(j, r):
                act.wait_ge(s_hp, j + 1)
                A(hT[:, r, :], PS[:, 4 + r, 0:P], ACT.Copy).then_inc(s_ht, 1)

            def rows_t(j, r):
                act.wait_ge(s_xtp, j + 1)
                A(xT[:, r, :], PS[:, r, 0:D], ACT.Copy).then_inc(s_xt, 1)

            tables(SILU)
            act.wait_ge(s_padt, 3)
            act.wait_ge(s_padrow, 1)
            pad_buckets(act, range(ACT_PADS))
            for b in range(SHARED_BEFORE):
                shared(b)

            def step(s, u):
                if not isinstance(s, int) or 2 <= s <= BLOCKS + 1:
                    silu(s - 2, u % 2)
                if not isinstance(s, int) or 3 <= s <= BLOCKS + 2:
                    hidden_t(s - 3, (u - 3) % 2)
                if not isinstance(s, int) or s < BLOCKS:
                    rows_t(s, u % 2)

            for s in range(NXS):
                step(s, s)
            with act.Fori(NXS, BLOCKS, NXS) as i:
                for u in range(NXS):
                    step(i + u, u)
            for s in range(BLOCKS, BLOCKS + 4):
                step(s, s)
            for b in range(SHARED_BEFORE, B):
                shared(b)
            for n in range(NT):
                summed(act, n)
                act.dma_start(out_d[n], resid[:, n, :]).then_inc(s_out[n % 4], 16)
            for q in range(4):
                act.wait_ge(s_out[q], 16 * (NT // 4))

        @block.vector
        def _(dve):
            c = Chain(dve, s_dve)
            V = nc.vector
            TT, TSC, STT = V.tensor_tensor, V.tensor_scalar, V.scalar_tensor_tensor
            M, AD, SU = ALU.mult, ALU.add, ALU.subtract

            def stats(src, b, st, mv, s_out):
                for t in range(TS):
                    c.add(V.bn_stats(st[:, b, t, :], src[:, b * TS + t, :]))
                c.wait()
                for t in range(TS):
                    ins = V.bn_aggr(mv[:, b, t, :], st[:, b, t, :])
                ins.then_inc(s_out, 1)

            def ln1_stats(b):
                dve.wait_ge(s_x[b], 16)
                stats(resid, b, st1, mv1, s_stats1)

            def ln1_rows(b):
                dve.wait_ge(s_rstd1, b + 1)
                at_least(dve, s_xntp, b)
                for t in range(TS):
                    ins = TSC(XN[:, t * D:(t + 1) * D], resid[:, b * TS + t, :], mv1[:, b, t, 0:1], rs1[:, b, 1, t:t + 1], SU, M)
                ins.then_inc(s_xn, 1)

            def turns(b):
                dve.wait_ge(s_step, b + 1)
                at_least(dve, s_trig, b)
                c.add(V.tensor_tensor_scan(TURN[:, SEQ:], TURN[:, 0:SEQ], TURN[:, 0:SEQ], 0.0, AD, ALU.bypass))
                c.wait()
                c.add(TSC(AB[:], TURN[:], MAGIC, None, AD))
                c.wait()
                c.add(STT(FR, AB[:], MAGIC, TURN[:], SU, SU))
                c.wait()
                TSC(AB[:].bitcast(i32), FR.bitcast(i32), 0x7FFFFFFF, None, ALU.bitwise_and).then_inc(s_turn, 1)

            def z_parts(b):
                p = b % 2
                s, co = SN[p][:, 0:SEQ], CS[p][:, 0:SEQ]
                dve.wait_ge(s_trig, b + 1)
                dve.wait_ge(s_rho, 2 * b + 2)
                c.add(STT(Q, s, 2.0, RHO2, M, M))
                c.wait()
                c.add(TT(W1, Q, s, M))
                c.add(TT(Q, Q, co, M))
                dve.wait_ge(s_dve, c.n - 1)
                c.add(STT(ZR, W1, 1.0, RHO2, AD, SU))
                STT(M2, W1, 2.0, E2, M, AD).then_inc(s_m2, 1)

            def z_sum(b):
                dve.wait_ge(s_zabs, b + 1)
                c.wait()
                STT(M2, ZR, 0.0, M2, ALU.max, AD).then_inc(s_zt, 1)

            def gate_input(b):
                p = b % 2
                dve.wait_ge(s_zroot, b + 1)
                dve.wait_ge(s_xh, 2 * b + 2)
                at_least(dve, s_outp, b)
                c.add(TT(Q, Q, RR, M))
                c.add(TT(T[0], XH[p][:, 0:SEQ], GX[p], M))
                ins = TT(T[1], XH[p][:, SEQ:], GX[p], M)
                ins.then_inc(s_xused, 1)
                c.wait()
                c.add(TT(T[2], T[0], SR, M))
                c.add(TT(T[5], T[0], Q, M))
                dve.wait_ge(s_xused, b + 1)
                c.add(TT(T[3], T[1], Q, M))
                c.add(TT(T[4], T[1], SR, M))
                dve.wait_ge(s_dve, c.n - 1)
                c.add(TT(T[2], T[2], T[3], AD))
                dve.wait_ge(s_dve, c.n - 1)
                c.add(TT(T[4], T[4], T[5], SU))

            def rotate_back(b):
                p = b % 2
                s, co = SN[p][:, SEQ:], CS[p][:, SEQ:]
                c.wait()
                c.add(TT(T[0], T[2], co, M))
                c.add(TT(T[1], T[4], s, M))
                c.add(TT(T[3], T[4], co, M))
                c.add(TT(T[5], T[2], s, M))
                dve.wait_ge(s_dve, c.n - 2)
                c.add(TT(T[0], T[0], T[1], AD))
                dve.wait_ge(s_dve, c.n - 1)
                c.add(TT(T[3], T[3], T[5], SU))

            def scan_rotate(b):
                p = b % 2
                s, co = SN[p][:, SEQ:], CS[p][:, SEQ:]
                c.wait()
                c.add(V.tensor_tensor_scan(T[6], RHO[p], T[0], 0.0, M, AD))
                c.add(V.tensor_tensor_scan(T[7], RHO[p], T[3], 0.0, M, AD))
                dve.wait_ge(s_dve, c.n - 1)
                TT(T[1], T[6], co, M)
                TT(T[4], T[6], s, M)
                c.wait()
                TT(T[2], T[7], s, M)
                TT(T[5], T[7], co, M).then_inc(s_prod, 1)

            def residual1(b):
                dve.wait_ge(s_outp, b + 1)
                dve.wait_ge(s_bout, b + 1)
                TT(resid[:, tiles(b), :], resid[:, tiles(b), :],
                   PS[:, 6:8, :].rearrange("p a (c d) -> p (a c) d", d=D), AD).then_inc(s_x1, 1)
                dve.wait_ge(s_x1, b + 1)
                stats(resid, b, st2, mv2, s_stats2)

            def ln2_rows(b):
                dve.wait_ge(s_rstd2, b + 1)
                if b >= 2:
                    dve.wait_ge(s_scat[b - 2], 16 * TS * TOPK)
                for t in range(TS):
                    ins = TSC(PAY[b % 2][:, t, 0, 0:D], resid[:, b * TS + t, :],
                              mv2[:, b, t, 0:1], rs2[:, b, 1, t:t + 1], SU, M)
                ins.then_inc(s_pay, 1)

            def choose(b):
                dve.wait_ge(s_sc, b + 1)
                c.add(V.tensor_reduce(gm[:], sc[:, :, :].rearrange("p t (g m) -> p t g m", m=PER), X, ALU.max))
                c.wait()
                for t in range(TS):
                    c.add(V.max(gv[:, t, :], gm[:, t, :]))
                c.wait()
                for t in range(TS):
                    c.add(V.max_index(gi[:, t, :], gv[:, t, :], gm[:, t, :]))
                c.wait()
                c.add(V.tensor_copy(gif[:], gi[:, :, 0:TOPG]))
                c.wait()
                for t in range(TS):
                    c.add(TT(geq[:, t, :, :], iota_g[:].unsqueeze(2).to_broadcast([P, GRP, TOPG]),
                             gif[:, t, :].unsqueeze(1).to_broadcast([P, GRP, TOPG]), ALU.is_equal))
                c.wait()
                c.add(V.tensor_reduce(gmask[:], geq[:], X, ALU.max))
                c.wait()
                c.add(TSC(gmm[:], gmask[:], 1.0, None, SU))
                tg = TS * GRP
                c.add(TT(msk[:].rearrange("p t (g m) -> p (t g) m", m=PER), sc[:].rearrange("p t (g m) -> p (t g) m", m=PER),
                         gmask[:].rearrange("p t g -> p (t g)").unsqueeze(2).to_broadcast([P, tg, PER]), M))
                c.wait()
                c.add(TT(msk[:].rearrange("p t (g m) -> p (t g) m", m=PER), msk[:].rearrange("p t (g m) -> p (t g) m", m=PER),
                         gmm[:].rearrange("p t g -> p (t g)").unsqueeze(2).to_broadcast([P, tg, PER]), AD))
                c.wait()
                for t in range(TS):
                    c.add(V.max(ev[:, t, :], msk[:, t, :]))
                c.wait()
                for t in range(TS):
                    c.add(V.max_index(ei[:, t, :], ev[:, t, :], msk[:, t, :]))
                c.add(V.tensor_reduce(wsum[:, 0, :], ev[:, :, 0:TOPK], X, AD))
                c.wait()
                c.add(V.tensor_copy(eif[:], ei[:, :, 0:TOPK]))
                c.add(V.reciprocal(wsum[:, 1, :], wsum[:, 0, :]))
                dve.wait_ge(s_dve, c.n - 1)
                c.add(TT(oh[:], iota_e[:].unsqueeze(1).to_broadcast([P, TS * TOPK, E]),
                         eif[:].rearrange("p t k -> p (t k)").unsqueeze(2).to_broadcast([P, TS * TOPK, E]), ALU.is_equal))
                c.wait()
                V.tensor_reduce(memb[:], oh[:].rearrange("p (t k) e -> p t e k", k=TOPK), X, ALU.max).then_inc(s_memb, 1)
                c.add(STT(PAY[b % 2][:, :, :, D + 1], ev[:, :, 0:TOPK], ROUTE_SCALE,
                          wsum[:, 1, :].unsqueeze(2).to_broadcast([P, TS, TOPK]), M, M))

            def places(b):
                dve.wait_ge(s_posp, b + 1)
                if b == 0:
                    c.add(V.tensor_copy(cb[:], cb0[:]))
                c.wait()
                c.add(TT(dpos[:], PS[:, 3, 0:TS * E].rearrange("p (t e) -> p t e", e=E),
                         cb[:].unsqueeze(1).to_broadcast([P, TS, E]), AD))
                c.wait()
                c.add(TT(cb[:], cb[:], PS[:, 3, TS * E:TS * E + E], AD))
                for t in range(TS):
                    c.add(TT(oh[:, t * TOPK:(t + 1) * TOPK, :], oh[:, t * TOPK:(t + 1) * TOPK, :],
                             dpos[:, t, :].unsqueeze(1).to_broadcast([P, TOPK, E]), M))
                c.wait()
                c.add(V.tensor_reduce(destf[:], oh[:], X, AD))
                c.wait()
                V.tensor_copy(dest[:, b % 2, :], destf[:]).then_inc(s_dest, 1)

            def channel_constants():
                dve.wait_ge(s_spout, 1)
                c.add(TT(ch[:, 6:7], ch[:, 7:8], ch[:, 5:6], AD))
                c.wait()
                TSC(ch[:, 1:2], ch[:, 6:7], -8.0, None, M)
                TSC(ch[:, 2:3], ch[:, 6:7], -16.0, None, M).then_inc(s_chan, 1)

            V.memset(cst[:, 0:1], math.pi / 2)
            V.memset(cst[:, 1:2], 1e-37)
            V.memset(cst[:, 2:3], EPS)
            V.memset(cst[:, 3:4], -LN2H)
            dve.wait_ge(s_chw, 16)
            TSC(ch[:, 3:4].bitcast(i32), chan_s[:, 4:5].bitcast(i32), 0x7FFFFFFF, None, ALU.bitwise_and).then_inc(s_spin, 1)
            TSC(ch[:, 0:1], chan_s[:, 5:6], 1.0 / (2 * math.pi), None, M)
            c.add(TSC(ch[:, 7:8], chan_s[:, 4:5], 0.0, None, ALU.max))
            for stage, b in (
                    (ln1_stats, 0), (ln1_rows, 0), (ln1_stats, 1), (ln1_stats, 2), (ln1_stats, 3), (ln1_rows, 1),
                    (ln1_rows, 2)):
                stage(b)
                if stage is ln1_stats and b == 0:
                    channel_constants()
            dve.wait_ge(s_small, 48)
            TSC(w_out_n[:], w_out_s[:, 0, :], -1.0, None, M).then_inc(s_chan, 1)
            dve.wait_ge(s_const, 9)
            for stage, b in (
                    (turns, 0), (z_parts, 0), (turns, 1), (z_sum, 0), (ln1_rows, 3), (gate_input, 0), (rotate_back, 0),
                    (scan_rotate, 0), (z_parts, 1), (turns, 2), (z_sum, 1), (residual1, 0), (gate_input, 1), (ln2_rows, 0),
                    (rotate_back, 1), (scan_rotate, 1), (choose, 0), (z_parts, 2), (places, 0), (z_sum, 2), (residual1, 1),
                    (gate_input, 2), (ln2_rows, 1), (rotate_back, 2), (scan_rotate, 2), (turns, 3), (choose, 1),
                    (z_parts, 3), (z_sum, 3), (places, 1), (residual1, 2), (gate_input, 3), (ln2_rows, 2),
                    (rotate_back, 3), (scan_rotate, 3), (choose, 2), (places, 2), (residual1, 3), (ln2_rows, 3),
                    (choose, 3), (places, 3)):
                stage(b)

            CN, CBK, CUM, LE, TMP = 0, 1, 2, 3, 4
            c.wait()
            V.tensor_copy(tabs[0:1, 2 * P:2 * P + E], cb[0:1, :]).then_inc(s_padrow, 1)
            c.add(TT(cnt[:, CN, :], cb[:], cb0[:], SU))
            c.wait()
            c.add(TT(cmpb, cnt[:, CN, :].unsqueeze(2).to_broadcast([P, E, NT]),
                     thr[:].unsqueeze(1).to_broadcast([P, E, NT]), ALU.is_gt))
            c.wait()
            c.add(V.tensor_reduce(cnt[:, CBK, :], cmpb, X, AD))
            c.wait()
            c.add(V.tensor_tensor_scan(cnt[:, CUM, :], cnt[:, CBK, :], zero_e[:], 0.0, AD, AD))
            c.wait()
            c.add(TSC(cnt[:, LE, :], cnt[:, CUM, :], iota_p[:, 0:1], None, ALU.is_le))
            c.wait()
            c.add(TT(cnt[:, TMP, :], cnt[:, LE, :], cnt[:, CBK, :], M))
            c.add(V.tensor_reduce(tabf[:, 0:1], cnt[:, LE, :], X, AD))
            c.wait()
            c.add(V.tensor_reduce(tabf[:, 1:2], cnt[:, TMP, :], X, AD))
            c.wait()
            c.add(TT(tabf[:, 1:2], iota_p[:], tabf[:, 1:2], SU))
            c.wait()
            c.add(TSC(tabf[:, 1:2], tabf[:, 1:2], float(P), None, M))
            c.wait()
            c.add(STT(tabf[:, 2:3], tabf[:, 0:1], float(CAP), tabf[:, 1:2], M, AD))
            c.wait()
            TSC(tabf[:, 2:3], tabf[:, 2:3], float(PADROW), None, ALU.min).then_inc(s_tabf, 1)
            TSC(tabf[:, 3:4], tabf[:, 0:1], float(E - 1), float(EW), ALU.min, M).then_inc(s_tabf, 1)
            dve.wait_ge(s_tabp, 1)
            V.tensor_copy(tabs[0:1, 0:2 * P], PS[0:1, 0, 0:2 * P]).then_inc(s_tab, 1)

            def shared_hidden(b):
                dve.wait_ge(s_shs, b + 1)
                TT(SHG[:].rearrange("p (h n) -> p h n", h=KD), SHG[:].rearrange("p (h n) -> p h n", h=KD),
                   PS[:, 4:6, :], M).then_inc(s_shh, 1)

            def shared_out(b):
                dve.wait_ge(s_shyp, b + 1)
                TT(resid[:, tiles(b), :], resid[:, tiles(b), :],
                   PS[:, 6:8, :].rearrange("p a (c d) -> p (a c) d", d=D), AD).then_inc(s_resid, 1)

            for b in range(SHARED_BEFORE):
                shared_hidden(b)
                shared_out(b)

            def hidden(j, r, slot):
                dve.wait_ge(s_sg, j + 1)
                STT(hh[:, r, :], sg[:, r, :], xs[:, slot, D + 1:D + 2], PS[:, 2 + r, P:2 * P], M, M).then_inc(s_hh, 1)

            def block_out(j, r, slot, scattered):
                dve.wait_ge(s_yp, j + 1)
                if scattered is not None:
                    dve.wait_ge(s_ys[slot], scattered)
                V.tensor_copy(yy[:, slot, :], PS[:, 6 + r, 0:D]).then_inc(s_y, 1)

            def step(s, u):
                fixed = isinstance(s, int)
                if not fixed or 2 <= s <= BLOCKS + 1:
                    hidden(s - 2, u % 2, (u - 2) % NXS)
                if not fixed or 4 <= s:
                    j = s - 4
                    if fixed:
                        scattered = 16 * (j // NY) if j >= NY else None
                    else:
                        scattered = (s - u) * (16 // NY) + 16 * ((u - 4) // NY)
                    block_out(j, u % 2, (u - 4) % NY, scattered)

            for s in range(NXS):
                step(s, s)
            with dve.Fori(NXS, BLOCKS, NXS) as i:
                for u in range(NXS):
                    step(i + u, u)
            for s in range(BLOCKS, BLOCKS + 4):
                step(s, s)
            for n in range(NT):
                late = n // TS + SHARED_BEFORE
                if n % TS == 0 and late < B:
                    shared_hidden(late)
                if not pool_sums(n):
                    sum_rows(dve, V, c, n)
                if n % TS == TS - 1 and late < B:
                    shared_out(late)

        @block.tensor
        def _(pe):
            mm = nc.tensor.matmul

            def ln1_transpose(b):
                pe.wait_ge(s_xn, b + 1)
                at_least(pe, s_xnt, b)
                at_least(pe, s_xn2, b - 2)
                for t in range(TS):
                    for k in range(KD):
                        ins = nc.tensor.transpose(PS[:, k, t * P:(t + 1) * P], XN[:, t * D + k * P:t * D + (k + 1) * P], ident[:])
                ins.then_inc(s_xntp, 1)

            def project(b):
                pe.wait_ge(s_xnt, b + 1)
                at_least(pe, s_xh, 2 * b)
                at_least(pe, s_dest, b - 2)
                at_least(pe, s_sc, b - 2)
                for m in range(KD):
                    for k in range(KD):
                        ins = mm(PS[:, 2 + m, :], w_in_s[:, k, m * P:(m + 1) * P], XNT[:, k * SEQ:(k + 1) * SEQ],
                                 start=(k == 0), stop=(k == KD - 1))
                ins.then_inc(s_xhp, 1)

            def gate(b):
                pe.wait_ge(s_xh, 2 * b + 2)
                at_least(pe, s_gates, 2 * b)
                for g in range(2):
                    for k in range(KD):
                        ins = mm(PS[:, 4 + g, :], bd[:, g, k, :], XH[b % 2][:, k * SEQ:(k + 1) * SEQ],
                                 start=(k == 0), stop=(k == KD - 1))
                ins.then_inc(s_gp, 1)

            def ln2_transpose(b):
                pe.wait_ge(s_pay, b + 1)
                pe.wait_ge(s_xnt, min(b + 3, B))
                at_least(pe, s_xn2, b)
                for t in range(TS):
                    for k in range(KD):
                        ins = nc.tensor.transpose(PS[:, k, t * P:(t + 1) * P], PAY[b % 2][:, t, 0, k * P:(k + 1) * P], ident[:])
                ins.then_inc(s_xn2p, 1)

            def logits(b):
                pe.wait_ge(s_xn2, b + 1)
                pe.wait_ge(s_xh, 2 * min(b + 3, B))
                at_least(pe, s_sc, b)
                for t in range(TS):
                    for k in range(KD):
                        ins = mm(PS[:, 2, t * E:(t + 1) * E], XN2T[:, b, k, t * P:(t + 1) * P], gwt_s[:, k, :],
                                 start=(k == 0), stop=(k == KD - 1))
                ins.then_inc(s_lgp, 1)

            def out_project(b):
                pe.wait_ge(s_prod, b + 1)
                at_least(pe, s_x1, b)
                parts = ((T[1], w_out_s[:, 0, :]), (T[2], w_out_n[:]), (T[4], w_out_s[:, 1, :]), (T[5], w_out_s[:, 1, :]))
                for t in range(TS):
                    for n, (h, w) in enumerate(parts):
                        ins = mm(PS[:, 6 + t // 2, (t % 2) * D:(t % 2 + 1) * D], h[:, t * P:(t + 1) * P], w,
                                 start=(n == 0), stop=(n == len(parts) - 1))
                ins.then_inc(s_outp, 1)

            def positions(b):
                pe.wait_ge(s_memb, b + 1)
                at_least(pe, s_dest, b)
                for t in range(TS):
                    for v in range(t + 1):
                        mm(PS[:, 3, t * E:(t + 1) * E], (tri if v == t else ones)[:], memb[:, v, :], start=(v == 0), stop=(v == t))
                for v in range(TS):
                    ins = mm(PS[:, 3, TS * E:TS * E + E], ones[:], memb[:, v, :], start=(v == 0), stop=(v == TS - 1))
                ins.then_inc(s_posp, 1)

            pe.wait_ge(s_const, 1)
            pe.wait_ge(s_win, 16)
            for stage, b in (
                    (ln1_transpose, 0), (project, 0), (ln1_transpose, 1)):
                stage(b)
            pe.wait_ge(s_gatew, 16)
            for stage, b in (
                    (gate, 0), (project, 1), (gate, 1), (ln1_transpose, 2), (project, 2), (gate, 2)):
                stage(b)
            pe.wait_ge(s_const, 9)
            pe.wait_ge(s_small, 48)
            pe.wait_ge(s_chan, 2)
            for stage, b in (
                    (out_project, 0), (ln2_transpose, 0), (logits, 0), (ln1_transpose, 3), (out_project, 1),
                    (positions, 0), (project, 3), (gate, 3), (ln2_transpose, 1), (logits, 1), (positions, 1),
                    (out_project, 2), (ln2_transpose, 2), (logits, 2), (out_project, 3), (positions, 2),
                    (ln2_transpose, 3), (logits, 3), (positions, 3)):
                stage(b)
            pe.wait_ge(s_tabf, 2)
            mm(PS[0:1, 0, 0:P], tabf[:, 2:3], ident[:], start=True, stop=True)
            mm(PS[0:1, 0, P:2 * P], tabf[:, 3:4], ident[:], start=True, stop=True).then_inc(s_tabp, 1)

            def shared(b):
                pe.wait_ge(s_dest, B)
                at_least(pe, s_shh, b)
                for h in range(KD):
                    for g in range(2):
                        for k in range(KD):
                            ins = mm(PS[:, 2 + 2 * g + h, :], sw13_s[:, k, g, h * P:(h + 1) * P], XN2T[:, b, k, :],
                                     start=(k == 0), stop=(k == KD - 1))
                ins.then_inc(s_shgp, 1)
                pe.wait_ge(s_shh, b + 1)
                at_least(pe, s_resid, b)
                for t in range(TS):
                    for h in range(KD):
                        ins = mm(PS[:, 6 + t // 2, (t % 2) * D:(t % 2 + 1) * D], SHG[:, h * SEQ + t * P:h * SEQ + (t + 1) * P],
                                 sw2_s[:, h, :], start=(h == 0), stop=(h == KD - 1))
                ins.then_inc(s_shyp, 1)

            pe.wait_ge(s_shw, 32)
            for b in range(SHARED_BEFORE):
                shared(b)
            pe.wait_ge(s_resid, SHARED_BEFORE)
            pe.wait_ge(s_tab, 1)
            pe.wait_ge(s_wearly, 16)
            pe.wait_ge(s_wlate, 16)

            def expert_of(j):
                reg = pe.alloc_register()
                pe.reg_load(reg, tabs[0:1, bass.ds(j + P, 1)])
                return pe.snap(reg, donate=True, min_val=0, max_val=(E - 1) * EW)

            def rows_t(j, r, slot, loads):
                pe.wait_ge(s_xs[slot], loads)
                for k in range(KD):
                    ins = nc.tensor.transpose(PS[:, r, k * P:(k + 1) * P], xs[:, slot, k * P:(k + 1) * P], ident[:])
                ins.then_inc(s_xtp, 1)

            def gate_up(j, r, w):
                pe.wait_ge(s_xt, j + 1)
                for k in range(KD):
                    ins = mm(PS[:, 2 + r, 0:2 * P], xT[:, r, k * P:(k + 1) * P], W[:, bass.ds(w + k * 2 * P, 2 * P)],
                             start=(k == 0), stop=(k == KD - 1))
                ins.then_inc(s_gup, 1)

            def hidden_t(j, r):
                pe.wait_ge(s_hh, j + 1)
                nc.tensor.transpose(PS[:, 4 + r, 0:P], hh[:, r, :], ident[:]).then_inc(s_hp, 1)

            def down(j, r, w):
                pe.wait_ge(s_ht, j + 1)
                if isinstance(j, int) and j == BLOCKS - 1:
                    pe.wait_ge(s_y, j - 1)
                mm(PS[:, 6 + r, 0:D], hT[:, r, :], W[:, bass.ds(w + KD * 2 * P, D)], start=True, stop=True).then_inc(s_yp, 1)

            def step(s, u, at):
                fixed = isinstance(s, int)
                if not fixed or 2 <= s <= BLOCKS + 1:
                    gate_up(s - 2, u % 2, at[u] if u in at else expert_of(s - 2))
                if not fixed or 3 <= s <= BLOCKS + 2:
                    hidden_t(s - 3, (u - 3) % 2)
                if not fixed or 4 <= s:
                    down(s - 4, u % 2, at[u - 2] if u - 2 in at else expert_of(s - 4))
                if not fixed or s < BLOCKS:
                    loads = 16 * (s // NXS + 1) if fixed else (s - u) * (16 // NXS) + 16
                    rows_t(s, u % 2, u % NXS, loads)
                if not fixed or 1 <= s <= BLOCKS:
                    at[u + 1] = expert_of(s - 1)

            at = {}
            for s in range(NXS):
                step(s, s, at)
            with pe.Fori(NXS, BLOCKS, NXS) as i:
                at = {}
                for u in range(NXS):
                    step(i + u, u, at)
            at = {}
            for s in range(BLOCKS, BLOCKS + 4):
                step(s, s, at)
            pe.wait_ge(s_y, BLOCKS)
            for b in range(SHARED_BEFORE, B):
                shared(b)


_LAUNCH = ["x", "chan", "w_in", "gate_bd", "w_out", "b_out", "gate_wt", "experts", "sw13", "sw2"]


def kernel(**inputs):
    import numpy as _np
    import concourse.bacc as _bacc
    from concourse import mybir as _mybir
    from concourse.bass_utils import run_bass_kernel_spmd as _run

    a = {k: _np.asarray(v) for k, v in inputs.items()}
    P = 128
    chan = _np.stack([a["L0_attn_b_in"][:P], a["L0_attn_b_in"][P:], a["L0_attn_b_gx"].reshape(P), a["L0_attn_b_ga"].reshape(P),
                      a["L0_attn_a_real"], a["L0_attn_a_imag"]], axis=1)
    E, F, D = a["L0_ffn_w11"].shape
    K = D // P
    w13 = _np.stack([a["L0_ffn_w11"], a["L0_ffn_w33"]])
    w13 = w13.reshape(2, E, F, K, P).transpose(4, 1, 3, 0, 2).reshape(P, E, K * 2 * F)
    w2 = a["L0_ffn_w22"].transpose(2, 0, 1)
    sw13 = _np.stack([a["L0_ffn_sw1"], a["L0_ffn_sw3"]])
    sw13 = sw13.reshape(2, sw13.shape[1], K, P).transpose(3, 2, 0, 1)
    sw2 = a["L0_ffn_sw2"].T.reshape(K, P, D).transpose(1, 0, 2)
    H, GI, GO = a["L0_attn_W_gx"].shape
    bd = _np.zeros((P, 2, K, P), a["L0_attn_W_gx"].dtype)
    for g, name in enumerate(("L0_attn_W_gx", "L0_attn_W_ga")):
        for h in range(H):
            k, r = divmod(h * GI, P)
            bd[r:r + GI, g, k, h * GO:(h + 1) * GO] = a[name][h]
    laid = dict(x=a["L0_attn_x"], chan=chan, w_in=a["L0_attn_W_in"], gate_bd=bd,
                w_out=a["L0_attn_W_out"], b_out=a["L0_attn_b_out"],
                gate_wt=a["L0_ffn_gate_w"].T.reshape(K, P, E).transpose(1, 0, 2),
                experts=_np.concatenate([w13, w2], axis=2), sw13=sw13, sw2=sw2)
    nc = _bacc.Bacc("TRN2", target_bir_lowering=False, num_devices=1)
    arrays, args = {}, []
    for name in _LAUNCH:
        v = _np.ascontiguousarray(laid[name])
        arrays[f"in_{name}"] = v
        args.append(nc.dram_tensor(f"in_{name}", v.shape, _mybir.dt.from_np(v.dtype), kind="ExternalInput").ap())
    shape = a["L0_attn_x"].shape
    args.append(nc.dram_tensor("out_0", shape, _mybir.dt.float32, kind="ExternalOutput").ap())
    preln_recurrence_moe(nc, *args)
    r = _run(nc, [arrays], core_ids=[0])
    return r.results[0]["out_0"]
```
